# Optimizing a Trainium2 kernel written in Bass

```python
import numpy as np
import jax
import jax.numpy as jnp

def _softmax(x, axis=-1):
    return jax.nn.softmax(x, axis=axis)

def _gelu(x):
    return jax.nn.gelu(x, approximate=True)

def _silu(x):
    return jax.nn.silu(x)

def _sigmoid(x):
    return jax.nn.sigmoid(x)

def _layernorm(x, axis=-1, eps=1e-05):
    m = jnp.mean(x, axis=axis, keepdims=True)
    v = jnp.var(x, axis=axis, keepdims=True)
    return (x - m) / jnp.sqrt(v + eps)

def _scatter_add(tgt, idx, src, axis=0):
    return tgt.at[idx].add(src)

def _segment_sum(src, seg, n):
    return jax.ops.segment_sum(src, seg, n)
kernel_name = 'mk_macaron_d1_jaxref_r8_20af90'

def setup_inputs(seed: int=0):
    np.random.seed(seed)
    _w = jnp.asarray

    def _L0_attn_setup():
        import jax, jax.numpy as jnp
        import numpy as np
        D_MODEL = 128
        NUM_HEADS = 4
        EXPAND_K = 1.0
        EXPAND_V = 2.0
        KEY_DIM = int(D_MODEL * EXPAND_K)
        VALUE_DIM = int(D_MODEL * EXPAND_V)
        HEAD_K = KEY_DIM // NUM_HEADS
        HEAD_V = VALUE_DIM // NUM_HEADS
        CHUNK = 64
        EPS = 1e-05
        ROPE_BASE = 10000.0

        def _apply_rotary(q, k):
            d = q.shape[-1]
            half = d // 2
            inv_freq = 1.0 / ROPE_BASE ** (jnp.arange(0, d, 2, dtype=jnp.float32) / d)
            t = jnp.arange(q.shape[1], dtype=jnp.float32)
            freqs = t[:, None] * inv_freq[None, :]
            cos = jnp.cos(freqs)[None, :, None, :]
            sin = jnp.sin(freqs)[None, :, None, :]

            def rot(x):
                x1, x2 = (x[..., :half], x[..., half:])
                return jnp.concatenate([x1 * cos - x2 * sin, x2 * cos + x1 * sin], axis=-1)
            return (rot(q), rot(k))

        def _chunk_retention(q, k, v, gamma):
            B, T, H, dk = q.shape
            dv = v.shape[-1]
            C = CHUNK
            N = T // C
            qc = q.reshape(B, N, C, H, dk).transpose(1, 0, 3, 2, 4)
            kc = k.reshape(B, N, C, H, dk).transpose(1, 0, 3, 2, 4)
            vc = v.reshape(B, N, C, H, dv).transpose(1, 0, 3, 2, 4)
            i = jnp.arange(C, dtype=jnp.float32)
            cross_dec = gamma[:, None] ** (i + 1.0)
            k_dec = gamma[:, None] ** (C - 1.0 - i)
            diff = i[:, None] - i[None, :]
            mask = jnp.where(diff >= 0, gamma[:, None, None] ** diff, 0.0)
            gC = gamma ** C

            def step(S, inp):
                qb, kb, vb = inp
                attn = jnp.einsum('bhid,bhjd->bhij', qb, kb) * mask
                o_intra = jnp.einsum('bhij,bhjv->bhiv', attn, vb)
                o_inter = jnp.einsum('bhid,bhdv->bhiv', qb * cross_dec[:, :, None], S)
                S_new = gC[:, None, None] * S + jnp.einsum('bhjd,bhjv->bhdv', kb * k_dec[:, :, None], vb)
                return (S_new, o_intra + o_inter)
            S0 = jnp.zeros((B, H, dk, dv), dtype=q.dtype)
            _, o = jax.lax.scan(step, S0, (qc, kc, vc))
            return o.transpose(1, 0, 3, 2, 4).reshape(B, T, H, dv)
        key = jax.random.key(seed)
        ks = jax.random.split(key, 7)
        B, T = (4, 256)
        s = 0.02
        return {'x': jax.random.normal(ks[0], (B, T, D_MODEL), dtype=jnp.float32), 'Wq': jax.random.normal(ks[1], (KEY_DIM, D_MODEL), dtype=jnp.float32) * s, 'Wk': jax.random.normal(ks[2], (KEY_DIM, D_MODEL), dtype=jnp.float32) * s, 'Wv': jax.random.normal(ks[3], (VALUE_DIM, D_MODEL), dtype=jnp.float32) * s, 'Wg': jax.random.normal(ks[4], (VALUE_DIM, D_MODEL), dtype=jnp.float32) * s, 'Wo': jax.random.normal(ks[5], (D_MODEL, VALUE_DIM), dtype=jnp.float32) * s, 'gnorm_w': jnp.ones((HEAD_V,), dtype=jnp.float32)}
    _L0_attn_in = _L0_attn_setup()

    def _L0_ffn_setup():
        import jax, jax.numpy as jnp
        import numpy as np
        E, D, F, GATE_DIM = (8, 128, 512, 16)
        B, T = (2, 256)
        key = jax.random.key(seed)
        ks = jax.random.split(key, 7)
        s = 0.02
        return {'hidden_states': jax.random.normal(ks[0], (B, T, D), dtype=jnp.float32), 'w_red': jax.random.normal(ks[1], (D, GATE_DIM), dtype=jnp.float32) * s, 'wg': jax.random.normal(ks[2], (E, GATE_DIM), dtype=jnp.float32), 'w1': jax.random.normal(ks[3], (E, D, F), dtype=jnp.float32) * s, 'b1': jax.random.normal(ks[4], (E, F), dtype=jnp.float32) * s, 'w2': jax.random.normal(ks[5], (E, F, D), dtype=jnp.float32) * s, 'b2': jax.random.normal(ks[6], (E, D), dtype=jnp.float32) * s}
    _L0_ffn_in = _L0_ffn_setup()
    _d = {'L0_attn_x': _L0_attn_in['x'], 'L0_attn_Wq': _L0_attn_in['Wq'], 'L0_attn_Wk': _L0_attn_in['Wk'], 'L0_attn_Wv': _L0_attn_in['Wv'], 'L0_attn_Wg': _L0_attn_in['Wg'], 'L0_attn_Wo': _L0_attn_in['Wo'], 'L0_attn_gnorm_w': _L0_attn_in['gnorm_w'], 'L0_ffn_w_red': _L0_ffn_in['w_red'], 'L0_ffn_wg': _L0_ffn_in['wg'], 'L0_ffn_w1': _L0_ffn_in['w1'], 'L0_ffn_b1': _L0_ffn_in['b1'], 'L0_ffn_w2': _L0_ffn_in['w2'], 'L0_ffn_b2': _L0_ffn_in['b2']}
    _x0 = _d['L0_attn_x']
    _d['L0_attn_x'] = jax.random.normal(jax.random.fold_in(jax.random.key(seed), 1), (8, 256, 128), dtype=_x0.dtype)
    del _x0
    return _d

def reference(L0_attn_x, L0_attn_Wq, L0_attn_Wk, L0_attn_Wv, L0_attn_Wg, L0_attn_Wo, L0_attn_gnorm_w, L0_ffn_w_red, L0_ffn_wg, L0_ffn_w1, L0_ffn_b1, L0_ffn_w2, L0_ffn_b2):

    def _L0_attn_ref(x, Wq, Wk, Wv, Wg, Wo, gnorm_w):
        import jax, jax.numpy as jnp
        import numpy as np
        D_MODEL = 128
        NUM_HEADS = 4
        EXPAND_K = 1.0
        EXPAND_V = 2.0
        KEY_DIM = int(D_MODEL * EXPAND_K)
        VALUE_DIM = int(D_MODEL * EXPAND_V)
        HEAD_K = KEY_DIM // NUM_HEADS
        HEAD_V = VALUE_DIM // NUM_HEADS
        CHUNK = 64
        EPS = 1e-05
        ROPE_BASE = 10000.0

        def _apply_rotary(q, k):
            d = q.shape[-1]
            half = d // 2
            inv_freq = 1.0 / ROPE_BASE ** (jnp.arange(0, d, 2, dtype=jnp.float32) / d)
            t = jnp.arange(q.shape[1], dtype=jnp.float32)
            freqs = t[:, None] * inv_freq[None, :]
            cos = jnp.cos(freqs)[None, :, None, :]
            sin = jnp.sin(freqs)[None, :, None, :]

            def rot(x):
                x1, x2 = (x[..., :half], x[..., half:])
                return jnp.concatenate([x1 * cos - x2 * sin, x2 * cos + x1 * sin], axis=-1)
            return (rot(q), rot(k))

        def _chunk_retention(q, k, v, gamma):
            B, T, H, dk = q.shape
            dv = v.shape[-1]
            C = CHUNK
            N = T // C
            qc = q.reshape(B, N, C, H, dk).transpose(1, 0, 3, 2, 4)
            kc = k.reshape(B, N, C, H, dk).transpose(1, 0, 3, 2, 4)
            vc = v.reshape(B, N, C, H, dv).transpose(1, 0, 3, 2, 4)
            i = jnp.arange(C, dtype=jnp.float32)
            cross_dec = gamma[:, None] ** (i + 1.0)
            k_dec = gamma[:, None] ** (C - 1.0 - i)
            diff = i[:, None] - i[None, :]
            mask = jnp.where(diff >= 0, gamma[:, None, None] ** diff, 0.0)
            gC = gamma ** C

            def step(S, inp):
                qb, kb, vb = inp
                attn = jnp.einsum('bhid,bhjd->bhij', qb, kb) * mask
                o_intra = jnp.einsum('bhij,bhjv->bhiv', attn, vb)
                o_inter = jnp.einsum('bhid,bhdv->bhiv', qb * cross_dec[:, :, None], S)
                S_new = gC[:, None, None] * S + jnp.einsum('bhjd,bhjv->bhdv', kb * k_dec[:, :, None], vb)
                return (S_new, o_intra + o_inter)
            S0 = jnp.zeros((B, H, dk, dv), dtype=q.dtype)
            _, o = jax.lax.scan(step, S0, (qc, kc, vc))
            return o.transpose(1, 0, 3, 2, 4).reshape(B, T, H, dv)
        B, T, _ = x.shape
        H = NUM_HEADS
        q = (x @ Wq.T).reshape(B, T, H, HEAD_K)
        k = (x @ Wk.T).reshape(B, T, H, HEAD_K)
        v = (x @ Wv.T).reshape(B, T, H, HEAD_V)
        g = (x @ Wg.T).reshape(B, T, H, HEAD_V)
        q, k = _apply_rotary(q, k)
        q = q * HEAD_K ** (-0.5)
        gamma = 1.0 - jnp.exp2(-5.0 - jnp.arange(H, dtype=jnp.float32))
        o = _chunk_retention(q, k, v, gamma)
        var = jnp.mean(o * o, axis=-1, keepdims=True)
        o = o * jax.lax.rsqrt(var + EPS) * gnorm_w
        o = o * (g * jax.nn.sigmoid(g))
        return o.reshape(B, T, H * HEAD_V) @ Wo.T

    def _L0_ffn_ref(hidden_states, w_red, wg, w1, b1, w2, b2):
        import jax, jax.numpy as jnp
        import numpy as np
        E, D, F, GATE_DIM = (8, 128, 512, 16)
        B, T = (2, 256)
        b, t, c = hidden_states.shape
        x = hidden_states.reshape(-1, c)
        red = x @ w_red
        wg_n = wg / jnp.maximum(jnp.linalg.norm(wg, axis=1, keepdims=True), 0.0001)
        logits = red @ wg_n.T
        gates = jax.nn.softmax(logits, axis=1)
        idx = jnp.argmax(gates, axis=1)
        scores = jnp.take_along_axis(gates, idx[:, None], axis=1)
        h = jax.nn.gelu(jnp.einsum('td,edf->etf', x, w1) + b1[:, None, :], approximate=False)
        y = jnp.einsum('etf,efd->etd', h, w2) + b2[:, None, :]
        out = jnp.take_along_axis(y, idx[None, :, None], axis=0)[0]
        out = out * scores
        return out.reshape(b, t, c)
    x = L0_attn_x
    x = x + 0.5 * _L0_ffn_ref(_layernorm(x, axis=-1), L0_ffn_w_red, L0_ffn_wg, L0_ffn_w1, L0_ffn_b1, L0_ffn_w2, L0_ffn_b2)
    x = x + _L0_attn_ref(_layernorm(x, axis=-1), L0_attn_Wq, L0_attn_Wk, L0_attn_Wv, L0_attn_Wg, L0_attn_Wo, L0_attn_gnorm_w)
    x = x + 0.5 * _L0_ffn_ref(_layernorm(x, axis=-1), L0_ffn_w_red, L0_ffn_wg, L0_ffn_w1, L0_ffn_b1, L0_ffn_w2, L0_ffn_b2)
    return x

_drawn_inputs = setup_inputs


def setup_inputs(seed=0):
    import zlib

    import numpy as np

    out = dict(_drawn_inputs(seed))
    spreads = {'L0_attn_gnorm_w': (1.0, 0.6)}
    factors = {'L0_ffn_w_red': 6.243,
     'L0_ffn_wg': 6.213,
     'L0_ffn_w1': 6.384,
     'L0_ffn_b1': 8.0,
     'L0_ffn_w2': 6.251,
     'L0_ffn_b2': 8.0}
    for name, (base, spread) in spreads.items():
        noise = np.random.default_rng([zlib.crc32(name.encode()), seed]).standard_normal(out[name].shape)
        drawn = base * np.exp(spread * noise) if base else spread * noise
        out[name] = jnp.asarray(drawn.astype(out[name].dtype))
    for name, factor in factors.items():
        out[name] = (out[name] * factor).astype(out[name].dtype)
    return out
```

```python
from contextlib import ExitStack

import numpy as np

import concourse.bass as bass
from concourse import mybir

F32 = mybir.dt.float32
F16 = mybir.dt.float16
I32 = mybir.dt.int32
U32 = mybir.dt.uint32
ALU = mybir.AluOpType
ACT = mybir.ActivationFunctionType
AX = mybir.AxisListType

P = 128
SEQS, T, D = 8, 256, 128
TOKENS = SEQS * T
NT = TOKENS // P
TPS = T // P
E, F, GATE = 8, 512, 16
NF = F // P
NS = (TOKENS + E * (P - 1)) // P
HEADS, DK, DV = 4, 32, 64
VD = HEADS * DV
EPS = 1e-5
ROW_SCALE = 16.0
WEIGHT_SCALE = 64.0
UNSCALE = 1.0 / (ROW_SCALE * WEIGHT_SCALE)
RSQRT_MAGIC = float(0x5F3759DF)
NEWTON_STEPS = 3

C_THRESH = 0
C_IOTA_E = C_THRESH + NT
C_IOTA_S = C_IOTA_E + E
C_BEFORE = C_IOTA_S + NS
C_TOKEN = C_BEFORE + E * E
C_COLS = C_TOKEN + NT


def rope_tables():
    inv_freq = (1.0 / np.float32(10000.0) ** (np.arange(0, DK, 2, dtype=np.float32) / np.float32(DK))).astype(np.float32)
    angle = (np.arange(T, dtype=np.float32)[:, None] * inv_freq[None, :]).astype(np.float64)
    cos = np.tile(np.cos(angle).T, (2 * HEADS, 1))
    sin = np.tile(np.concatenate([-np.sin(angle).T, np.sin(angle).T]), (HEADS, 1))
    gamma = 1.0 - 2.0 ** (-5.0 - np.arange(HEADS))
    grow = np.repeat(gamma[:, None] ** np.arange(T)[None, :], DK, axis=0)
    q_factor = grow * DK ** -0.5 * UNSCALE
    k_factor = UNSCALE / grow
    table = np.stack([cos * q_factor, cos * k_factor, sin * q_factor, sin * k_factor], axis=1)
    return np.ascontiguousarray(table.reshape(P, 4 * T).astype(np.float32))


def small_constants():
    table = np.zeros((P, C_COLS), np.float32)
    table[:, C_THRESH:C_IOTA_E] = P * np.arange(NT)
    table[:, C_IOTA_E:C_IOTA_S] = np.arange(E)
    table[:, C_IOTA_S:C_BEFORE] = np.arange(NS)
    e = np.arange(E)
    table[:, C_BEFORE:C_TOKEN] = (e[None, :] < e[:, None]).astype(np.float32).reshape(-1)
    table[:, C_TOKEN:] = P * np.arange(NT)[None, :] + np.arange(P)[:, None]
    return table


def half_constants():
    i = np.arange(P)
    tile, expert = i // E, i % E
    parts = [
        i[:, None] == i[None, :],
        i[:, None] < i[None, :],
        (expert[:, None] == expert[None, :]) & (tile[:, None] < tile[None, :]),
        np.tile(i, (P, 1)),
        np.ones((P, P)),
        expert[:, None] == np.arange(E)[None, :],
    ]
    return np.concatenate([np.asarray(p, np.float16) for p in parts], axis=1)


def causal_mask():
    i = np.arange(P)
    causal = (i[:, None] <= i[None, :]).astype(np.float32)
    return np.concatenate([np.eye(P, dtype=np.float32), causal, np.ones((P, P), np.float32), causal], axis=1)

class Counter:

    def __init__(self, engine, sem, step=1):
        self.engine, self.sem, self.step, self.count = engine, sem, step, 0

    def mark(self, instruction):
        instruction.then_inc(self.sem, self.step)
        self.count += self.step
        return (self.sem, self.count)

    def wait(self, *marks):
        for m in marks:
            if m is not None:
                self.engine.wait_ge(*m)


def macaron(nc, x, w_proj, w_o, gnorm, w_redT, wg, w1, b1T, w2, b2, rope, consts, halves, masks, out):
    ctx = ExitStack()
    with ctx:
        ctx.enter_context(nc.allow_low_precision("float16 parts are exact splits"))

        def sb(name, shape, dt=F32):
            return ctx.enter_context(nc.sbuf_tensor(name, shape, dt))

        def ring(name, n, shape, dt=F32):
            return [sb(f"{name}{i}", shape, dt) for i in range(n)]

        def sem(name):
            return ctx.enter_context(nc.semaphore(name))

        def dma_counters(name, n):
            return [Counter(None, sem(f"{name}{i}"), 16) for i in range(n)]

        pe = Counter(nc.tensor, sem("tensor_done"))
        dve = Counter(nc.vector, sem("vector_done"))
        act = Counter(nc.scalar, sem("scalar_done"))
        pool = Counter(nc.gpsimd, sem("pool_done"))
        sp = nc.sync

        banks = [ctx.enter_context(nc.psum_tensor(f"bank{i}", [P, 512], F32)) for i in range(8)]
        emptied = [None] * 8

        c32 = sb("c32", [P, C_COLS])
        c16 = sb("c16", [P, 5 * P + E], F16)
        mask_sb = sb("mask_sb", [P, 4 * P])
        rope_sb = sb("rope_sb", [P, 4 * T])
        ident16, before16, tile_before16, iota16, ones16 = (c16[:, k * P:(k + 1) * P] for k in range(5))
        expert16 = c16[:, 5 * P:5 * P + E]
        ident32, score_mask = mask_sb[:, 0:P], mask_sb[:, P:4 * P]

        x_sb = sb("x_sb", [P, NT, D])
        row_stats = sb("row_stats", [P, NT, 6])
        row_mean_var = sb("row_mean_var", [P, NT, 2])
        xnT = sb("xnT", [P, 2, TOKENS], F16)
        w_proj32 = sb("w_proj32", [P, 4 * P + 2 * VD])
        w_proj16 = sb("w_proj16", [P, 2, 4 * P + 2 * VD], F16)
        w_o_sb = sb("w_o_sb", [P, 2, D])
        gnorm_sb = sb("gnorm_sb", [P, 1])
        w_redT_sb = sb("w_redT_sb", [GATE, D])
        wg_sb = sb("wg_sb", [E, GATE])
        w_stage = sb("w_stage", [P, 2, E * F])
        w1_16 = [sb(f"w1_16_{k}", [P, E * F], F16) for k in range(2)]
        w2_16 = [sb(f"w2_16_{k}", [P, E * F], F16) for k in range(2)]
        b1_sb = sb("b1_sb", [P, E * NF])
        b2_sb = sb("b2_sb", [P, E * D])

        rows_dram = [nc.dram_tensor(f"rows{k}", [TOKENS, 2 * D], F16) for k in range(2)]
        y_dram = [nc.dram_tensor(f"y{k}", [NS * P, D], F32) for k in range(2)]

        def load(name, dst, src):
            return Counter(None, sem(f"load_{name}"), 16).mark(sp.dma_start(dst, src))

        LOADS = 4
        x_tiles = x.rearrange("(t p) d -> p t d", p=P)
        x_in = []
        for g in range(LOADS):
            n = NT // LOADS
            x_in.append(load(f"x{g}", x_sb[:, g * n:(g + 1) * n, :], x_tiles[:, g * n:(g + 1) * n, :]))
            if g == 0:
                wg_in = load("wg", wg_sb[:, :], wg)
                w_redT_in = load("w_redT", w_redT_sb[:, :], w_redT)
                masks_in = load("masks", mask_sb[:, :], masks)
                halves_in = load("halves", c16[:, :], halves)
        W_PARTS = 4
        ep = E // W_PARTS
        w1_in, w2_in = [], []
        for g in range(W_PARTS):
            cols = slice(g * ep * F, (g + 1) * ep * F)
            w1_in.append(load(f"w1_{g}", w_stage[:, 0, cols].rearrange("p (e f) -> p e f", e=ep),
                              w1[g * ep:(g + 1) * ep].rearrange("e d f -> d e f")))
        consts_in = load("consts", c32[:, :], consts)
        b1_in = load("b1", b1_sb[:, :], b1T)
        for g in range(W_PARTS):
            cols = slice(g * ep * F, (g + 1) * ep * F)
            w2_in.append(load(f"w2_{g}", w_stage[:, 1, cols].rearrange("p (m d) -> p m d", d=D),
                              w2[g * ep:(g + 1) * ep].rearrange("e (j p) d -> p (e j) d", p=P)))
        b2_in = load("b2", b2_sb[:, :], b2.rearrange("(o e) d -> o (e d)", o=1).broadcast_to([P, E * D]))
        proj_in = load("w_proj", w_proj32[:, :], w_proj)
        wo_in = load("w_o", w_o_sb[:, :, :], w_o.rearrange("(k p) d -> p k d", p=P))
        gnorm_in = load("gnorm", gnorm_sb[:, :], gnorm)
        rope_in = load("rope", rope_sb[:, :], rope)

        rs_val, rs_tmp, rs_out = sb("rs_val", [P, NT]), sb("rs_tmp", [P, NT]), sb("rs_out", [P, NT])
        rs_int = sb("rs_int", [P, NT], I32)

        def rsqrt_steps(n, ready, out_read):
            v, t, y, i = rs_val[:, 0:n], rs_tmp[:, 0:n], rs_out[:, 0:n], rs_int[:, 0:n]
            dve.wait(ready)
            m = dve.mark(dve.engine.tensor_scalar(i, v.bitcast(I32), 1, None, ALU.logical_shift_right))
            yield m
            dve.wait(m, out_read)
            m = dve.mark(dve.engine.tensor_scalar(y.bitcast(I32), i, -1.0, RSQRT_MAGIC, ALU.mult, ALU.add))
            yield m
            for _ in range(NEWTON_STEPS):
                dve.wait(m)
                m = dve.mark(dve.engine.tensor_tensor(t, y, v, ALU.mult))
                yield m
                dve.wait(m)
                m = dve.mark(dve.engine.scalar_tensor_tensor(t, t, -0.5, y, ALU.mult, ALU.mult))
                yield m
                dve.wait(m)
                m = dve.mark(dve.engine.scalar_tensor_tensor(y, t, 1.5, y, ALU.add, ALU.mult))
                yield m

        gate_sq = sb("gate_sq", [E, GATE])
        gate_ss = sb("gate_ss", [E, 1])
        gate_wn = sb("gate_wn", [E, GATE])
        gate_wnT = sb("gate_wnT", [GATE, E])
        gate_w32 = sb("gate_w32", [P, E])
        gate_w16 = sb("gate_w16", [P, 2, E], F16)

        def gate_weights():
            dve.wait(wg_in)
            m = dve.mark(dve.engine.tensor_tensor(gate_sq[:, :], wg_sb[:, :], wg_sb[:, :], ALU.mult))
            dve.wait(m)
            m = dve.mark(dve.engine.tensor_reduce(gate_ss[:, :], gate_sq[:, :], AX.X, ALU.add))
            ones = dve.mark(dve.engine.memset(rs_val[:, :], 1.0))
            dve.wait(ones)
            m = dve.mark(dve.engine.tensor_scalar(rs_val[0:E, 0:1], gate_ss[:, :], 1e-8, None, ALU.max))
            *_, m = rsqrt_steps(1, m, None)
            dve.wait(m)
            scaled = dve.mark(dve.engine.tensor_scalar(gate_wn[:, :], wg_sb[:, :], rs_out[0:E, 0:1], None, ALU.mult))
            pe.wait(scaled, masks_in)
            bank = banks[7]
            m = pe.mark(pe.engine.transpose(bank[0:GATE, 0:E], gate_wn[:, :], ident32[0:E, 0:E]))
            act.wait(m)
            m = act.mark(act.engine.activation(gate_wnT[:, :], bank[0:GATE, 0:E], ACT.Copy))
            pe.wait(m, w_redT_in)
            bank = banks[6]
            emptied[7] = m
            m = pe.mark(pe.engine.matmul(bank[:, 0:E], w_redT_sb[:, :], gate_wnT[:, :], start=True, stop=True))
            act.wait(m)
            m = act.mark(act.engine.activation(gate_w32[:, :], bank[:, 0:E], ACT.Copy, scale=WEIGHT_SCALE))
            emptied[6] = m
            act.wait(m)
            m = act.mark(act.engine.activation(gate_w16[:, 0, :], gate_w32[:, :], ACT.Copy))
            pool.wait(m)
            return pool.mark(pool.engine.tensor_tensor(gate_w16[:, 1, :], gate_w32[:, :], gate_w16[:, 0, :], ALU.subtract)), scaled

        def split_weights(hi, lo, src, loaded):
            act.wait(loaded)
            scaled = act.mark(act.engine.activation(src, src, ACT.Copy, scale=WEIGHT_SCALE))
            act.wait(scaled)
            m = act.mark(act.engine.activation(hi, src, ACT.Copy))
            pool.wait(m)
            return pool.mark(pool.engine.tensor_tensor(lo, src, hi, ALU.subtract))

        def layernorm_stats(tiles, ready):
            marks = []
            for t, m in zip(tiles, ready):
                dve.wait(m)
                marks.append(dve.mark(dve.engine.bn_stats(row_stats[:, t, :], x_sb[:, t, :])))
            for t, m in zip(tiles, marks):
                dve.wait(m)
                m = dve.mark(dve.engine.bn_aggr(row_mean_var[:, t, :], row_stats[:, t, :]))
            return m

        def layernorm_value(col, t0, n, stats_ready, val_read):
            k = ROW_SCALE ** -2
            dve.wait(stats_ready, val_read)
            return dve.mark(dve.engine.tensor_scalar(rs_val[:, col:col + n], row_mean_var[:, t0:t0 + n, 1],
                                                     k, EPS * k, ALU.mult, ALU.add))

        ROW_BUFS = 4
        xn32 = ring("xn32_", ROW_BUFS, [P, TPS, D])
        xn16 = ring("xn16_", ROW_BUFS, [P, TPS, 2, D], F16)
        rows_store = dma_counters("rows_stored", ROW_BUFS)
        xn32_read = [None] * ROW_BUFS
        xn16_transposed = [None] * ROW_BUFS
        xn16_stored = [None] * ROW_BUFS

        def normalise(seq, buf, col, rs_ready):
            n32 = xn32[buf]
            dve.wait(rs_ready, xn32_read[buf])
            for j in range(TPS):
                t = TPS * seq + j
                m = dve.mark(dve.engine.tensor_scalar(n32[:, j, :], x_sb[:, t, :], row_mean_var[:, t, 0:1],
                                                      rs_out[:, col + j:col + j + 1], ALU.subtract, ALU.mult))
            return m

        def split_rows(buf, normalised, lo_engine):
            n32, n16 = xn32[buf], xn16[buf]
            act.wait(normalised, xn16_transposed[buf], xn16_stored[buf])
            hi = act.mark(act.engine.activation(n16[:, :, 0, :], n32[:, :, :], ACT.Copy))
            lo_engine.wait(hi)
            lo = lo_engine.mark(lo_engine.engine.tensor_tensor(n16[:, :, 1, :], n32[:, :, :], n16[:, :, 0, :], ALU.subtract))
            xn32_read[buf] = lo
            return lo

        def store_rows(k, seq, buf, split):
            sp.wait_ge(*split)
            rows = rows_dram[k].ap().rearrange("(t p) c -> p t c", p=P)[:, TPS * seq:TPS * (seq + 1), :]
            xn16_stored[buf] = rows_store[buf].mark(
                sp.dma_start(rows, xn16[buf][:, :, :, :].rearrange("p t h d -> p t (h d)")))
            return xn16_stored[buf]

        xnT_read = [None] * SEQS

        def transpose_rows(seq, buf, split, b):
            n16 = xn16[buf]
            b16 = banks[b][:, :].bitcast(F16)
            pe.wait(split, halves_in, emptied[b])
            for h in range(2):
                for j in range(TPS):
                    c = (h * TPS + j) * P
                    m = pe.engine.transpose(b16[:, c:c + P], n16[:, j, h, :], ident16)
            m = pe.mark(m)
            xn16_transposed[buf] = m
            act.wait(m, xnT_read[seq])
            m = act.mark(act.engine.activation(xnT[:, :, seq * T:(seq + 1) * T],
                                               b16[:, 0:2 * T].rearrange("p (h t) -> p h t", h=2), ACT.Copy))
            emptied[b] = m
            return m

        logits = sb("logits", [P, NT, E])

        def gate_logits(seq, xT_ready, w_ready, b, logits_read):
            bank = banks[b]
            pe.wait(xT_ready, w_ready, emptied[b])
            for j in range(TPS):
                t = TPS * seq + j
                hi, lo = xnT[:, 0, t * P:(t + 1) * P], xnT[:, 1, t * P:(t + 1) * P]
                o = bank[:, j * E:(j + 1) * E]
                pe.engine.matmul(o, hi, gate_w16[:, 0, :], start=True, stop=False)
                pe.engine.matmul(o, hi, gate_w16[:, 1, :], start=False, stop=False)
                m = pe.engine.matmul(o, lo, gate_w16[:, 0, :], start=False, stop=True)
            m = pe.mark(m)
            xnT_read[seq] = m
            act.wait(m, logits_read)
            m = act.mark(act.engine.activation(logits[:, TPS * seq:TPS * (seq + 1), :],
                                               bank[:, 0:TPS * E].rearrange("p (t e) -> p t e", e=E),
                                               ACT.Copy, scale=UNSCALE))
            emptied[b] = m
            return m

        shape_te = [P, NT, E]
        r_max = sb("r_max", [P, NT])
        r_shift = sb("r_shift", shape_te)
        r_exp = sb("r_exp", shape_te)
        r_sum = sb("r_sum", [P, NT])
        half_score = [sb(f"half_score{k}", [P, NT]) for k in range(2)]
        r_cand = sb("r_cand", shape_te)
        r_expert = sb("r_expert", [P, NT])
        member = sb("member", shape_te, F16)
        count16 = sb("count16", [P, P], F16)
        r_rank = sb("r_rank", shape_te)
        r_total = sb("r_total", [P, E])
        r_cmp = sb("r_cmp", [P, E, NT])
        r_tiles = sb("r_tiles", [P, E])
        r_tri = sb("r_tri", [P, E, E])
        r_start = sb("r_start", [P, E])
        r_start_slot = sb("r_start_slot", [P, E])
        r_posf = sb("r_posf", [P, NT])
        slot_of = [sb(f"slot_of{k}", [P, NT], U32) for k in range(2)]
        r_posi = sb("r_posi", [P, NT], I32)
        r_rowi = sb("r_rowi", [P, NT], I32)
        r_tilei = sb("r_tilei", [P, NT], I32)
        r_rowf = sb("r_rowf", [P, NT])
        r_tilef = sb("r_tilef", [P, NT])
        row_hot = sb("row_hot", [P, NT, P], F16)
        tile_hot = sb("tile_hot", [P, NT, NS])
        tile_token = sb("tile_token", [P, NT, NS], F16)
        token_of = [sb(f"token_of{k}", [P, NS], U32) for k in range(2)]
        s_cmp = sb("s_cmp", [1, NS, E - 1])
        s_expert = sb("s_expert", [1, NS])
        offsets = [sb(f"offsets{k}", [1, 3, NS], I32) for k in range(2)]
        OFF_W, OFF_B1, OFF_B2 = range(3)

        def route(k, logits_ready):
            v = dve.engine

            def step(instruction):
                m = dve.mark(instruction)
                dve.wait(m)
                return m

            def over_experts(a):
                return a.unsqueeze(2).broadcast_to(shape_te)

            dve.wait(logits_ready, consts_in)
            step(v.tensor_reduce(r_max[:, :], logits[:, :, :], AX.X, ALU.max))
            shifted = step(v.tensor_tensor(r_shift[:, :, :], logits[:, :, :], over_experts(r_max[:, :]), ALU.subtract))
            act.wait(shifted)
            exps = act.mark(act.engine.activation(r_exp[:, :, :], r_shift[:, :, :], ACT.Exp))
            iota_e = c32[:, C_IOTA_E:C_IOTA_S].unsqueeze(1).broadcast_to(shape_te)
            step(v.tensor_scalar(r_cand[:, :, :], r_shift[:, :, :], 0.0, float(E), ALU.is_lt, ALU.mult))
            step(v.tensor_tensor(r_cand[:, :, :], r_cand[:, :, :], iota_e, ALU.add))
            step(v.tensor_reduce(r_expert[:, :], r_cand[:, :, :], AX.X, ALU.min))
            m = step(v.tensor_tensor(member[:, :, :], iota_e, over_experts(r_expert[:, :]), ALU.is_equal))
            members = member[:, :, :].rearrange("p t e -> p (t e)")
            counts, ranks, tokens = banks[0], banks[1], banks[2]
            pe.wait(m, emptied[0])
            m = pe.mark(pe.engine.matmul(counts[:, 0:P], members, ones16, start=True, stop=True))
            dve.wait(m)
            m = dve.mark(v.tensor_copy(count16[:, :], counts[:, 0:P]))
            emptied[0] = m
            pe.wait(m, emptied[1])
            pe.engine.matmul(ranks[:, P:P + E], count16[:, :], expert16, start=True, stop=True)
            pe.engine.matmul(ranks[:, 0:P], before16, members, start=True, stop=False)
            ranked = pe.mark(pe.engine.matmul(ranks[:, 0:P], count16[:, :], tile_before16, start=False, stop=True))
            dve.wait(exps)
            step(v.tensor_reduce(r_sum[:, :], r_exp[:, :, :], AX.X, ALU.add))
            inverse = dve.mark(v.reciprocal(half_score[k][:, :], r_sum[:, :]))
            dve.wait(ranked)
            step(v.tensor_copy(r_total[:, :], ranks[:, P:P + E]))
            thresholds = c32[:, C_THRESH:C_IOTA_E].unsqueeze(1).broadcast_to([P, E, NT])
            step(v.tensor_tensor(r_cmp[:, :, :], r_total[:, :].unsqueeze(2).broadcast_to([P, E, NT]), thresholds, ALU.is_gt))
            step(v.tensor_reduce(r_tiles[:, :], r_cmp[:, :, :], AX.X, ALU.add))
            before = c32[:, C_BEFORE:C_TOKEN].rearrange("p (a b) -> p a b", a=E)
            step(v.tensor_tensor(r_tri[:, :, :], r_tiles[:, :].unsqueeze(1).broadcast_to([P, E, E]), before, ALU.mult))
            started = step(v.tensor_reduce(r_start[:, :], r_tri[:, :, :], AX.X, ALU.add))
            step(v.tensor_scalar(r_start_slot[:, :], r_start[:, :], float(P), None, ALU.mult))
            m = step(v.tensor_tensor(r_rank[:, :, :], ranks[:, 0:P].rearrange("p (t e) -> p t e", e=E),
                                     r_start_slot[:, :].unsqueeze(1).broadcast_to(shape_te), ALU.add))
            emptied[1] = m
            step(v.tensor_tensor(r_rank[:, :, :], r_rank[:, :, :], member[:, :, :], ALU.mult))
            step(v.tensor_reduce(r_posf[:, :], r_rank[:, :, :], AX.X, ALU.add))
            step(v.tensor_copy(r_posi[:, :], r_posf[:, :]))
            dve.mark(v.tensor_scalar(r_rowi[:, :], r_posi[:, :], P - 1, None, ALU.bitwise_and))
            split_pos = dve.mark(v.tensor_scalar(r_tilei[:, :], r_posi[:, :], 7, None, ALU.logical_shift_right))
            iota_s = c32[0:1, C_IOTA_S:C_BEFORE].unsqueeze(2).broadcast_to([1, NS, E - 1])
            starts = r_start[0:1, 1:E].unsqueeze(1).broadcast_to([1, NS, E - 1])
            dve.wait(started)
            compared = dve.mark(v.tensor_tensor(s_cmp[:, :, :], starts, iota_s, ALU.is_le))
            dve.wait(split_pos)
            dve.mark(v.tensor_copy(r_rowf[:, :], r_rowi[:, :]))
            located = dve.mark(v.tensor_copy(r_tilef[:, :], r_tilei[:, :]))
            dve.wait(compared)
            experts_known = dve.mark(v.tensor_reduce(s_expert[:, :], s_cmp[:, :, :], AX.X, ALU.add))
            shape_ts = [P, NT, NS]
            iota_ts = c32[:, C_IOTA_S:C_BEFORE].unsqueeze(1).broadcast_to(shape_ts)
            dve.wait(located)
            hot = dve.mark(v.tensor_tensor(tile_hot[:, :, :], iota_ts, r_tilef[:, :].unsqueeze(2).broadcast_to(shape_ts), ALU.is_equal))
            dve.wait(experts_known)
            for row, unit in ((OFF_W, F), (OFF_B1, NF), (OFF_B2, D)):
                offsets_ready = dve.mark(v.tensor_scalar(offsets[k][:, row, :], s_expert[:, :], float(unit), None, ALU.mult))
            dve.wait(hot)
            dve.mark(v.tensor_tensor(tile_token[:, :, :], tile_hot[:, :, :],
                                     c32[:, C_TOKEN:C_COLS].unsqueeze(2).broadcast_to(shape_ts), ALU.mult))
            pe.wait(emptied[2])
            for t in range(NT):
                m = dve.mark(v.tensor_scalar(row_hot[:, t, :], iota16, r_rowf[:, t:t + 1], None, ALU.is_equal))
                pe.wait(m)
                m = pe.engine.matmul(tokens[:, 0:NS], row_hot[:, t, :], tile_token[:, t, :], start=(t == 0), stop=(t == NT - 1))
            m = pe.mark(m)
            dve.wait(inverse)
            step(v.tensor_scalar(half_score[k][:, :], half_score[k][:, :], 0.5, None, ALU.mult))
            slots_ready = dve.mark(v.tensor_copy(slot_of[k][:, :], r_posf[:, :]))
            dve.wait(m)
            tokens_ready = dve.mark(v.tensor_copy(token_of[k][:, :], tokens[:, 0:NS]))
            emptied[2] = tokens_ready
            return slots_ready, tokens_ready, offsets_ready

        GATHERS, SLOTS_T, HIDDEN, RESULTS = 8, 3, 3, 4
        slot_rows = ring("slot_rows", GATHERS, [P, 2, D], F16)
        gather_done = dma_counters("gathered", GATHERS)
        slotT = ring("slotT", SLOTS_T, [P, 2, P], F16)
        hidden32 = ring("hidden32_", HIDDEN, [P, NF, P])
        hidden16 = ring("hidden16_", HIDDEN, [P, 2, NF, P], F16)
        y_sb = ring("y_sb", RESULTS, [P, D])
        y_store = dma_counters("y_stored", RESULTS)
        BANK_T, BANK_UP, BANK_DOWN = (0, 1), (2, 3, 4), (5, 6)
        gathered, transposed, t_copied, up_done, activated, hidden_split, down_done, y_stored = ({} for _ in range(8))

        def load_offsets(eng, k, row, limit, ready):
            regs = [eng.engine.alloc_register(f"off{k}_{row}_{i}") for i in range(NS)]
            eng.wait(ready)
            eng.engine.reg_load(regs, offsets[k][0:1, row, :])
            return [eng.engine.snap(r, min_val=0, max_val=limit) for r in regs]

        def experts(k, rows_stored, tokens_ready, offsets_ready, w1_ready, w2_ready):
            s0, s1 = k * NS, (k + 1) * NS
            w_off = load_offsets(pe, k, OFF_W, (E - 1) * F, offsets_ready)
            b1_off = load_offsets(act, k, OFF_B1, (E - 1) * NF, offsets_ready)
            b2_off = load_offsets(dve, k, OFF_B2, (E - 1) * D, offsets_ready)
            pool.wait(tokens_ready, *rows_stored)
            pe.wait(w1_ready)
            act.wait(b1_in)
            dve.wait(b2_in)

            def gather(s):
                pool.wait(transposed.get(s - GATHERS))
                gathered[s] = gather_done[s % GATHERS].mark(pool.engine.indirect_dma_start(
                    slot_rows[s % GATHERS][:, :, :].rearrange("p h d -> p (h d)"), None, rows_dram[k].ap(),
                    bass.IndirectOffsetOnAxis(token_of[k][:, s - s0:s - s0 + 1], 0)))

            def transpose(s):
                rows, t16 = slot_rows[s % GATHERS], slotT[s % SLOTS_T]
                b = BANK_T[s % len(BANK_T)]
                b16 = banks[b][:, :].bitcast(F16)
                pe.wait(gathered[s], emptied[b])
                pe.engine.transpose(b16[:, 0:P], rows[:, 0, :], ident16)
                transposed[s] = pe.mark(pe.engine.transpose(b16[:, P:2 * P], rows[:, 1, :], ident16))
                act.wait(transposed[s], up_done.get(s - SLOTS_T))
                t_copied[s] = act.mark(act.engine.activation(t16[:, :, :], b16[:, 0:2 * P].rearrange("p (h t) -> p h t", h=2), ACT.Copy))
                emptied[b] = t_copied[s]

            def up(s):
                hi, lo = slotT[s % SLOTS_T][:, 0, :], slotT[s % SLOTS_T][:, 1, :]
                b = BANK_UP[s % len(BANK_UP)]
                pe.wait(t_copied[s], emptied[b])
                for f in range(NF):
                    o = banks[b][:, f * P:(f + 1) * P]
                    w_hi = w1_16[0][:, bass.ds(w_off[s - s0] + f * P, P)]
                    w_lo = w1_16[1][:, bass.ds(w_off[s - s0] + f * P, P)]
                    pe.engine.matmul(o, w_hi, hi, start=True, stop=False)
                    pe.engine.matmul(o, w_hi, lo, start=False, stop=False)
                    m = pe.engine.matmul(o, w_lo, hi, start=False, stop=True)
                up_done[s] = pe.mark(m)

            def activate(s):
                h = hidden32[s % HIDDEN]
                b = BANK_UP[s % len(BANK_UP)]
                act.wait(up_done[s], hidden_split.get(s - HIDDEN))
                for f in range(NF):
                    m = act.mark(act.engine.activation(h[:, f, :], banks[b][:, f * P:(f + 1) * P], ACT.Gelu,
                                                       bias=b1_sb[:, bass.ds(b1_off[s - s0] + f, 1)], scale=UNSCALE))
                activated[s] = emptied[b] = m

            def split(s):
                h, parts = hidden32[s % HIDDEN], hidden16[s % HIDDEN]
                dve.wait(activated[s], down_done.get(s - HIDDEN))
                m = dve.mark(dve.engine.tensor_copy(parts[:, 0, :, :], h[:, :, :]))
                dve.wait(m)
                hidden_split[s] = dve.mark(dve.engine.tensor_tensor(parts[:, 1, :, :], h[:, :, :], parts[:, 0, :, :], ALU.subtract))

            def down(s):
                parts = hidden16[s % HIDDEN]
                b = BANK_DOWN[s % len(BANK_DOWN)]
                o = banks[b][:, 0:D]
                pe.wait(hidden_split[s], emptied[b])
                for f in range(NF):
                    w_hi = w2_16[0][:, bass.ds(w_off[s - s0] + f * D, D)]
                    w_lo = w2_16[1][:, bass.ds(w_off[s - s0] + f * D, D)]
                    pe.engine.matmul(o, parts[:, 0, f, :], w_hi, start=(f == 0), stop=False)
                    pe.engine.matmul(o, parts[:, 0, f, :], w_lo, start=False, stop=False)
                    m = pe.engine.matmul(o, parts[:, 1, f, :], w_hi, start=False, stop=(f == NF - 1))
                down_done[s] = pe.mark(m)

            def finish(s):
                y = y_sb[s % RESULTS]
                b = BANK_DOWN[s % len(BANK_DOWN)]
                dve.wait(down_done[s], y_stored.get(s - RESULTS))
                m = dve.mark(dve.engine.scalar_tensor_tensor(y[:, :], banks[b][:, 0:D], 1.0 / WEIGHT_SCALE,
                                                             b2_sb[:, bass.ds(b2_off[s - s0], D)], ALU.mult, ALU.add))
                emptied[b] = m
                sp.wait_ge(*m)
                y_stored[s] = y_store[s % RESULTS].mark(sp.dma_start(y_dram[k].ap()[(s - s0) * P:(s - s0 + 1) * P, :], y[:, :]))

            T_AHEAD = SLOTS_T - 1
            for s in range(s0, s0 + GATHERS - 1):
                gather(s)
            for s in range(s0, s0 + T_AHEAD):
                transpose(s)
            for s in range(s0, s1 + 2):
                if s + GATHERS - 1 < s1:
                    gather(s + GATHERS - 1)
                if s + T_AHEAD < s1:
                    transpose(s + T_AHEAD)
                if s < s1:
                    up(s)
                    activate(s)
                if s == s0:
                    pe.wait(w2_ready)
                if s0 <= s - 2:
                    down(s - 2)
                if s0 <= s - 1 < s1:
                    split(s - 1)
                if s0 <= s - 2:
                    finish(s - 2)
            return [y_stored[s] for s in range(s1 - RESULTS, s1)]

        BACK = 6
        back = ring("back", BACK, [P, D])
        back_landed = dma_counters("back_landed", BACK)
        fetched, added_back = {}, {}

        def fetch(k, t):
            n = k * NT + t
            pool.wait(added_back.get(n - BACK))
            fetched[n] = back_landed[n % BACK].mark(pool.engine.indirect_dma_start(
                back[n % BACK][:, :], None, y_dram[k].ap(), bass.IndirectOffsetOnAxis(slot_of[k][:, t:t + 1], 0)))

        def add_back(k, t, x_ready=None):
            n = k * NT + t
            dve.wait(fetched[n], x_ready)
            added_back[n] = dve.mark(dve.engine.scalar_tensor_tensor(x_sb[:, t, :], back[n % BACK][:, :], half_score[k][:, t:t + 1],
                                                                     x_sb[:, t, :], ALU.mult, ALU.add))
            return added_back[n]

        gate_ready, rs_free = gate_weights()
        rows_stored = []
        group = NT // LOADS
        seqs = group // TPS
        w1_parts = [slice(g * ep * F, (g + 1) * ep * F) for g in range(W_PARTS)]
        for g in range(LOADS):
            tiles = range(g * group, (g + 1) * group)
            m = layernorm_stats(tiles, [x_in[g]] + [None] * (group - 1))
            m = layernorm_value(0, g * group, group, m, rs_free)
            *_, rs_ready = rsqrt_steps(group, m, rs_free)
            for seq in range(g * seqs, (g + 1) * seqs):
                buf = seq % ROW_BUFS
                normalised = normalise(seq, buf, TPS * seq - g * group, rs_ready)
                rs_free = normalised
                split = split_rows(buf, normalised, dve)
                rows_stored.append(store_rows(0, seq, buf, split))
                xT_ready = transpose_rows(seq, buf, split, seq % 4)
                logits_ready = gate_logits(seq, xT_ready, gate_ready, 4 + seq % 4, None)
            w1_ready = split_weights(w1_16[0][:, w1_parts[g]], w1_16[1][:, w1_parts[g]], w_stage[:, 0, w1_parts[g]], w1_in[g])
        slots_ready, tokens_ready, offsets_ready = route(0, logits_ready)
        for g in range(W_PARTS):
            w2_ready = split_weights(w2_16[0][:, w1_parts[g]], w2_16[1][:, w1_parts[g]], w_stage[:, 1, w1_parts[g]], w2_in[g])
        results_stored = experts(0, rows_stored, tokens_ready, offsets_ready, w1_ready, w2_ready)

        proj_ready = split_weights(w_proj16[:, 0, :], w_proj16[:, 1, :], w_proj32[:, :], proj_in)
        pool.wait(wo_in, gnorm_in)
        wo_ready = pool.mark(pool.engine.tensor_scalar(w_o_sb[:, :, :], w_o_sb[:, :, :], gnorm_sb[:, 0:1], None, ALU.mult))

        rot_tmp = ring("rot_tmp", 2, [P, 2, 2 * T])
        rotated = ring("rotated", 2, [P, 2 * T])
        values = ring("values", 3, [P, TPS, VD])
        silu_g = ring("silu_g", 3, [P, TPS, VD])
        weights = ring("weights", 2, [P, HEADS, 3 * P])
        squares = sb("squares", [P, TPS * VD])
        head_ss = sb("head_ss", [P, TPS * HEADS])
        gated = ring("gated", 2, [P, TPS, VD])
        gatedT = sb("gatedT", [P, 2, T])
        BANK_OUT, BANK_ROWS, BANK_ROWS2, BANK_MIX = 0, 1, 2, 7
        BANK_QK, BANK_VG = (3, 4), (5, 6)
        BANK_SCORE = (3, 4, 5, 6)
        COL_X1, COL_X2, COL_HEAD = 0, TPS, 2 * TPS
        RS_N = COL_HEAD + TPS * HEADS
        (split1, split2, xT_ready, qk_done, rotate_multiplied, rot_ready, v_ready, g_ready, scored,
         masked, mixed, squared, summed, heads_gated, gT_ready, projected_out) = ({} for _ in range(16))

        def mix(b):
            w, v, bank = weights[b % 2], values[b % 3], banks[BANK_MIX]
            pe.wait(masked[b], v_ready[b], emptied[BANK_MIX])
            for h in range(HEADS):
                hv = slice(h * DV, (h + 1) * DV)
                pe.engine.matmul(bank[:, h * DV:(h + 1) * DV], w[:, h, 0:P], v[:, 0, hv], start=True, stop=True)
                o = bank[:, VD + h * DV:VD + (h + 1) * DV]
                pe.engine.matmul(o, w[:, h, P:2 * P], v[:, 0, hv], start=True, stop=False)
                m = pe.engine.matmul(o, w[:, h, 2 * P:3 * P], v[:, 1, hv], start=False, stop=True)
            mixed[b] = pe.mark(m)
            act.wait(mixed[b], summed.get(b - 1))
            squared[b] = act.mark(act.engine.activation(squares[:, :], bank[:, :], ACT.Square))

        def transpose_heads(b):
            og, bank = gated[b % 2], banks[BANK_OUT]
            pe.wait(heads_gated[b], emptied[BANK_OUT])
            for c in range(2):
                for j in range(TPS):
                    m = pe.engine.transpose(bank[:, (c * TPS + j) * P:(c * TPS + j + 1) * P], og[:, j, c * P:(c + 1) * P], ident32)
            m = pe.mark(m)
            act.wait(m, projected_out.get(b - 1))
            gT_ready[b] = act.mark(act.engine.activation(gatedT[:, :, :], bank[:, :].rearrange("p (c t) -> p c t", c=2), ACT.Copy))

        def project_out(b):
            bank = banks[BANK_OUT]
            pe.wait(gT_ready[b])
            for j in range(TPS):
                for c in range(2):
                    m = pe.engine.matmul(bank[:, j * D:(j + 1) * D], gatedT[:, c, j * P:(j + 1) * P], w_o_sb[:, c, :],
                                         start=(c == 0), stop=(c == 1))
            projected_out[b] = pe.mark(m)

        def add_attention(b):
            dve.wait(projected_out[b])
            xs = x_sb[:, TPS * b:TPS * (b + 1), :].rearrange("p t d -> p (t d)")
            m = dve.mark(dve.engine.tensor_tensor(xs, banks[BANK_OUT][:, 0:TPS * D], xs, ALU.add))
            emptied[BANK_OUT] = m
            return m

        def project_qk(b):
            span = slice(b * T, (b + 1) * T)
            hi, lo = xnT[:, 0, span], xnT[:, 1, span]
            pe.wait(xT_ready[b])
            for swapped in range(2):
                bank = banks[BANK_QK[swapped]]
                pe.wait(emptied[BANK_QK[swapped]])
                for j in range(2):
                    c = (2 * j + swapped) * P
                    w_hi, w_lo = w_proj16[:, 0, c:c + P], w_proj16[:, 1, c:c + P]
                    o = bank[:, j * T:(j + 1) * T]
                    pe.engine.matmul(o, w_hi, hi, start=True, stop=False)
                    pe.engine.matmul(o, w_hi, lo, start=False, stop=False)
                    m = pe.engine.matmul(o, w_lo, hi, start=False, stop=True)
                qk_done[b, swapped] = pe.mark(m)

        def rotate(b):
            tmp, r = rot_tmp[b % 2], rotated[b % 2]
            dve.wait(rot_ready.get(b - 2))
            for j in range(2):
                dve.wait(qk_done[b, j])
                m = dve.mark(dve.engine.tensor_tensor(tmp[:, j, :], banks[BANK_QK[j]][:, :], rope_sb[:, j * 2 * T:(j + 1) * 2 * T], ALU.mult))
                emptied[BANK_QK[j]] = m
            pool.wait(m, scored.get(b - 2))
            rot_ready[b] = pool.mark(pool.engine.tensor_tensor(r[:, :], tmp[:, 0, :], tmp[:, 1, :], ALU.add))

        def project_vg(b):
            vg_hi, vg_lo = w_proj16[:, 0, 4 * P:], w_proj16[:, 1, 4 * P:]
            v, g = values[b % 3], silu_g[b % 3]
            act.wait(mixed.get(b - 3), heads_gated.get(b - 3))
            for j in range(TPS):
                bank = banks[BANK_VG[j]]
                c = b * T + j * P
                hi, lo = xnT[:, 0, c:c + P], xnT[:, 1, c:c + P]
                pe.wait(emptied[BANK_VG[j]])
                pe.engine.matmul(bank[:, :], hi, vg_hi, start=True, stop=False)
                pe.engine.matmul(bank[:, :], hi, vg_lo, start=False, stop=False)
                m = pe.mark(pe.engine.matmul(bank[:, :], lo, vg_hi, start=False, stop=True))
                act.wait(m)
                v_ready[b] = act.mark(act.engine.activation(v[:, j, :], bank[:, 0:VD], ACT.Copy, scale=UNSCALE))
                g_ready[b] = act.mark(act.engine.activation(g[:, j, :], bank[:, VD:2 * VD], ACT.Silu, scale=UNSCALE))
                emptied[BANK_VG[j]] = g_ready[b]
            xnT_read[b] = m

        def score(b):
            r = rotated[b % 2]
            pe.wait(rot_ready[b])
            for h in range(HEADS):
                hs = slice(h * DK, (h + 1) * DK)
                pe.wait(emptied[BANK_SCORE[h]])
                pe.engine.matmul(banks[BANK_SCORE[h]][:, 0:2 * P], r[hs, T:T + P], r[hs, 0:T], start=True, stop=True,
                                 tile_position=(h * DK, 0))
            for h in range(HEADS):
                hs = slice(h * DK, (h + 1) * DK)
                scored[b, h] = pe.mark(pe.engine.matmul(banks[BANK_SCORE[h]][:, 2 * P:3 * P], r[hs, T + P:2 * T], r[hs, P:T],
                                                        start=True, stop=True, tile_position=(h * DK, 0)))
            scored[b] = scored[b, HEADS - 1]

        def mask(b, h):
            dve.wait(scored[b, h])
            if h == 0:
                dve.wait(mixed.get(b - 2))
            m = dve.mark(dve.engine.tensor_tensor(weights[b % 2][:, h, :], banks[BANK_SCORE[h]][:, 0:3 * P], score_mask, ALU.mult))
            emptied[BANK_SCORE[h]] = masked[b] = m

        def head_sums(b, val_read):
            dve.wait(squared[b])
            summed[b] = dve.mark(dve.engine.tensor_reduce(head_ss[:, :], squares[:, :].rearrange("p (g d) -> p g d", d=DV),
                                                          AX.X, ALU.add))
            dve.wait(summed[b], val_read)
            return dve.mark(dve.engine.tensor_scalar(rs_val[:, COL_HEAD:RS_N], head_ss[:, :], 1.0 / DV, EPS, ALU.mult, ALU.add))

        def gate_heads(b, rs_ready, transposed_before):
            g, og, bank = silu_g[b % 3], gated[b % 2], banks[BANK_MIX]
            dve.wait(rs_ready, g_ready[b], transposed_before)
            grouped = [a.rearrange("p t (h d) -> p (t h) d", d=DV) for a in (g[:, :, :], og[:, :, :])]
            m = dve.mark(dve.engine.tensor_tensor(grouped[1], grouped[0],
                                                  rs_out[:, COL_HEAD:RS_N].unsqueeze(2).broadcast_to([P, TPS * HEADS, DV]), ALU.mult))
            dve.wait(m)
            m = dve.mark(dve.engine.tensor_tensor(og[:, :, :].rearrange("p t c -> p (t c)"), bank[:, :],
                                                  og[:, :, :].rearrange("p t c -> p (t c)"), ALU.mult))
            heads_gated[b] = emptied[BANK_MIX] = m

        LAG_PROJECT, LAG_SCORE, LAG_MIX, LAG_OUT, LAG_GATE = 1, 2, 3, 4, 5

        def now(i, lag):
            return i - lag if 0 <= i - lag < SEQS else None

        rows2_stored = []
        pool.wait(slots_ready, *results_stored)
        for j in range(TPS):
            fetch(0, j)
        pe.wait(proj_ready, wo_ready)
        dve.wait(rope_in)
        for i in range(SEQS + LAG_GATE):
            first, proj, sc, mx, last, gate = (now(i, lag) for lag in (0, LAG_PROJECT, LAG_SCORE, LAG_MIX, LAG_OUT, LAG_GATE))
            if i + 1 < SEQS:
                for j in range(TPS):
                    fetch(0, TPS * (i + 1) + j)
            if mx is not None:
                mix(mx)
            if last is not None:
                transpose_heads(last)
            if proj is not None:
                xT_ready[proj] = transpose_rows(proj, proj % 2, split1[proj], BANK_ROWS)
            if gate is not None:
                x2T_ready = transpose_rows(gate, 2 + gate % 2, split2[gate], BANK_ROWS2)
            if last is not None:
                project_out(last)
            if proj is not None:
                project_qk(proj)
            value = None
            if first is not None:
                added = [add_back(0, TPS * first + j) for j in range(TPS)]
                m = layernorm_stats(range(TPS * first, TPS * (first + 1)), added)
                value = layernorm_value(COL_X1, TPS * first, TPS, m, rs_free)
            if mx is not None:
                value = head_sums(mx, rs_free)
            if last is not None:
                m = add_attention(last)
                m = layernorm_stats(range(TPS * last, TPS * (last + 1)), [m] * TPS)
                value = layernorm_value(COL_X2, TPS * last, TPS, m, rs_free)
            if proj is not None:
                rotate(proj)
                project_vg(proj)
            if gate is not None:
                logits_ready = gate_logits(gate, x2T_ready, gate_ready, BANK_ROWS2, None)
            if sc is not None:
                score(sc)
            steps = rsqrt_steps(RS_N, value, rs_free) if value is not None else iter(())
            rs_ready = value
            if sc is not None:
                for h in range(HEADS):
                    for m in [next(steps, None), next(steps, None), next(steps, None)]:
                        rs_ready = m or rs_ready
                    mask(sc, h)
            for m in steps:
                rs_ready = m
            if mx is not None:
                gate_heads(mx, rs_ready, gT_ready.get(mx - 2))
                rs_free = heads_gated[mx]
            if first is not None:
                rs_free = normalise(first, first % 2, COL_X1, rs_ready)
                split1[first] = split_rows(first % 2, rs_free, pool)
            if last is not None:
                rs_free = normalise(last, 2 + last % 2, COL_X2, rs_ready)
                split2[last] = split_rows(2 + last % 2, rs_free, pool)
                rows2_stored.append(store_rows(1, last, 2 + last % 2, split2[last]))

        slots_ready, tokens_ready, offsets_ready = route(1, logits_ready)
        results_stored = experts(1, rows2_stored, tokens_ready, offsets_ready, None, None)
        out_tiles = out.rearrange("(t p) d -> p t d", p=P)
        out_store = Counter(None, sem("out_stored"), 16)
        pool.wait(slots_ready, *results_stored)
        for seq in range(SEQS):
            for j in range(TPS):
                fetch(1, TPS * seq + j)
            for j in range(TPS):
                m = add_back(1, TPS * seq + j)
            sp.wait_ge(*m)
            stored = out_store.mark(sp.dma_start(out_tiles[:, TPS * seq:TPS * (seq + 1), :], x_sb[:, TPS * seq:TPS * (seq + 1), :]))
        sp.wait_ge(*stored)


def kernel(**inputs):
    import concourse.bacc as bacc
    from concourse.bass_utils import run_bass_kernel_spmd

    a = {k: np.asarray(v) for k, v in inputs.items()}
    swap = np.arange(P).reshape(HEADS, 2, DK // 2)[:, ::-1].reshape(-1)
    wq, wk = a["L0_attn_Wq"], a["L0_attn_Wk"]
    arrays = {
        "x": a["L0_attn_x"].reshape(TOKENS, D),
        "w_proj": np.concatenate([wq, wq[swap], wk, wk[swap], a["L0_attn_Wv"], a["L0_attn_Wg"]]).T,
        "w_o": a["L0_attn_Wo"].T,
        "gnorm": np.tile(a["L0_attn_gnorm_w"], 2).reshape(P, 1),
        "w_redT": a["L0_ffn_w_red"].T,
        "wg": a["L0_ffn_wg"],
        "w1": a["L0_ffn_w1"],
        "b1T": a["L0_ffn_b1"].reshape(E * NF, P).T,
        "w2": a["L0_ffn_w2"],
        "b2": a["L0_ffn_b2"],
        "rope": rope_tables(),
        "consts": small_constants(),
        "halves": half_constants(),
        "masks": causal_mask(),
    }
    arrays = {k: np.ascontiguousarray(v) for k, v in arrays.items()}
    nc = bacc.Bacc("TRN2", target_bir_lowering=False, num_devices=1)
    args = [nc.dram_tensor(f"in_{k}", v.shape, mybir.dt.from_np(v.dtype), kind="ExternalInput").ap()
            for k, v in arrays.items()]
    out = nc.dram_tensor("out_x", (TOKENS, D), F32, kind="ExternalOutput").ap()
    macaron(nc, *args, out)
    r = run_bass_kernel_spmd(nc, [{f"in_{k}": v for k, v in arrays.items()}], core_ids=[0])
    return r.results[0]["out_x"].reshape(SEQS, T, D)
```

```python
from contextlib import ExitStack

import numpy as np

import concourse.bass as bass
from concourse import mybir

F32 = mybir.dt.float32
F16 = mybir.dt.float16
I32 = mybir.dt.int32
U32 = mybir.dt.uint32
ALU = mybir.AluOpType
ACT = mybir.ActivationFunctionType
AX = mybir.AxisListType

P = 128
SEQS, T, D = 8, 256, 128
TOKENS = SEQS * T
NT = TOKENS // P
TPS = T // P
E, F, GATE = 8, 512, 16
NF = F // P
NS = (TOKENS + E * (P - 1)) // P
HEADS, DK, DV = 4, 32, 64
VD = HEADS * DV
EPS = 1e-5
ROW_SCALE = 16.0
WEIGHT_SCALE = 64.0
UNSCALE = 1.0 / (ROW_SCALE * WEIGHT_SCALE)
RSQRT_MAGIC = float(0x5F3759DF)
NEWTON_STEPS = 3

C_THRESH = 0
C_IOTA_E = C_THRESH + NT
C_IOTA_S = C_IOTA_E + E
C_BEFORE = C_IOTA_S + NS
C_TOKEN = C_BEFORE + E * E
C_COLS = C_TOKEN + NT


def rope_tables():
    inv_freq = (1.0 / np.float32(10000.0) ** (np.arange(0, DK, 2, dtype=np.float32) / np.float32(DK))).astype(np.float32)
    angle = (np.arange(T, dtype=np.float32)[:, None] * inv_freq[None, :]).astype(np.float64)
    cos = np.tile(np.cos(angle).T, (2 * HEADS, 1))
    sin = np.tile(np.concatenate([-np.sin(angle).T, np.sin(angle).T]), (HEADS, 1))
    gamma = 1.0 - 2.0 ** (-5.0 - np.arange(HEADS))
    grow = np.repeat(gamma[:, None] ** np.arange(T)[None, :], DK, axis=0)
    q_factor = grow * DK ** -0.5 * UNSCALE
    k_factor = UNSCALE / grow
    table = np.stack([cos * q_factor, cos * k_factor, sin * q_factor, sin * k_factor], axis=1)
    return np.ascontiguousarray(table.reshape(P, 4 * T).astype(np.float32))


def small_constants():
    table = np.zeros((P, C_COLS), np.float32)
    table[:, C_THRESH:C_IOTA_E] = P * np.arange(NT)
    table[:, C_IOTA_E:C_IOTA_S] = np.arange(E)
    table[:, C_IOTA_S:C_BEFORE] = np.arange(NS)
    e = np.arange(E)
    table[:, C_BEFORE:C_TOKEN] = (e[None, :] < e[:, None]).astype(np.float32).reshape(-1)
    table[:, C_TOKEN:] = P * np.arange(NT)[None, :] + np.arange(P)[:, None]
    return table


def half_constants():
    i = np.arange(P)
    tile, expert = i // E, i % E
    parts = [
        i[:, None] == i[None, :],
        i[:, None] < i[None, :],
        (expert[:, None] == expert[None, :]) & (tile[:, None] < tile[None, :]),
        np.tile(i, (P, 1)),
        np.ones((P, P)),
        expert[:, None] == np.arange(E)[None, :],
    ]
    return np.concatenate([np.asarray(p, np.float16) for p in parts], axis=1)


def causal_mask():
    i = np.arange(P)
    causal = (i[:, None] <= i[None, :]).astype(np.float32)
    return np.concatenate([np.eye(P, dtype=np.float32), causal, np.ones((P, P), np.float32), causal,
                           (i[:, None] // DV == np.arange(P // DV)[None, :]).astype(np.float32)], axis=1)

class Counter:

    def __init__(self, engine, sem, step=1):
        self.engine, self.sem, self.step, self.count = engine, sem, step, 0

    def mark(self, instruction):
        instruction.then_inc(self.sem, self.step)
        self.count += self.step
        return (self.sem, self.count)

    def wait(self, *marks):
        for m in marks:
            if m is not None:
                self.engine.wait_ge(*m)


def macaron(nc, x, w_proj, w_o, gnorm, w_redT, wg, w1, b1T, w2, b2, rope, consts, halves, masks, out):
    ctx = ExitStack()
    with ctx:
        ctx.enter_context(nc.allow_low_precision("float16 parts are exact splits"))

        def sb(name, shape, dt=F32):
            return ctx.enter_context(nc.sbuf_tensor(name, shape, dt))

        def ring(name, n, shape, dt=F32):
            return [sb(f"{name}{i}", shape, dt) for i in range(n)]

        def sem(name):
            return ctx.enter_context(nc.semaphore(name))

        def dma_counters(name, n):
            return [Counter(None, sem(f"{name}{i}"), 16) for i in range(n)]

        pe = Counter(nc.tensor, sem("tensor_done"))
        dve = Counter(nc.vector, sem("vector_done"))
        act = Counter(nc.scalar, sem("scalar_done"))
        pool = Counter(nc.gpsimd, sem("pool_done"))
        sp = nc.sync

        banks = [ctx.enter_context(nc.psum_tensor(f"bank{i}", [P, 512], F32)) for i in range(8)]
        emptied = [None] * 8

        c32 = sb("c32", [P, C_COLS])
        c16 = sb("c16", [P, 5 * P + E], F16)
        mask_sb = sb("mask_sb", [P, 4 * P + 2])
        rope_sb = sb("rope_sb", [P, 4 * T])
        ident16, before16, tile_before16, iota16, ones16 = (c16[:, k * P:(k + 1) * P] for k in range(5))
        expert16 = c16[:, 5 * P:5 * P + E]
        ident32, score_mask, head_rows = mask_sb[:, 0:P], mask_sb[:, P:4 * P], mask_sb[:, 4 * P:]

        x_sb = sb("x_sb", [P, NT, D])
        row_stats = sb("row_stats", [P, NT, 6])
        row_mean_var = sb("row_mean_var", [P, NT, 2])
        xnT = sb("xnT", [P, 2, TOKENS], F16)
        w_proj32 = sb("w_proj32", [P, 4 * P + 2 * VD])
        w_proj16 = sb("w_proj16", [P, 2, 4 * P + 2 * VD], F16)
        w_o_sb = sb("w_o_sb", [P, 2, D])
        gnorm_sb = sb("gnorm_sb", [P, 1])
        w_redT_sb = sb("w_redT_sb", [GATE, D])
        wg_sb = sb("wg_sb", [E, GATE])
        w_stage = sb("w_stage", [P, 2, E * F])
        w1_16 = sb("w1_16", [P, E * NF * 2 * P], F16)
        w2_16 = sb("w2_16", [P, E * NF * 2 * D], F16)
        b1_sb = sb("b1_sb", [P, E * NF])
        b2_sb = sb("b2_sb", [P, E * D])

        rows_dram = [nc.dram_tensor(f"rows{k}", [TOKENS, 2 * D], F16) for k in range(2)]
        y_dram = [nc.dram_tensor(f"y{k}", [NS * P, D], F32) for k in range(2)]

        def load(name, dst, src):
            return Counter(None, sem(f"load_{name}"), 16).mark(sp.dma_start(dst, src))

        LOADS = 2
        x_tiles = x.rearrange("(t p) d -> p t d", p=P)
        x_in = []
        for g in range(LOADS):
            n = NT // LOADS
            x_in.append(load(f"x{g}", x_sb[:, g * n:(g + 1) * n, :], x_tiles[:, g * n:(g + 1) * n, :]))
            if g == 0:
                wg_in = load("wg", wg_sb[:, :], wg)
                w_redT_in = load("w_redT", w_redT_sb[:, :], w_redT)
                masks_in = load("masks", mask_sb[:, :], masks)
                halves_in = load("halves", c16[:, :], halves)
        W_PARTS = 4
        ep = E // W_PARTS
        w1_in, w2_in = [], []
        for g in range(W_PARTS):
            cols = slice(g * ep * F, (g + 1) * ep * F)
            w1_in.append(load(f"w1_{g}", w_stage[:, 0, cols].rearrange("p (e f) -> p e f", e=ep),
                              w1[g * ep:(g + 1) * ep].rearrange("e d f -> d e f")))
        consts_in = load("consts", c32[:, :], consts)
        b1_in = load("b1", b1_sb[:, :], b1T)
        for g in range(W_PARTS):
            cols = slice(g * ep * F, (g + 1) * ep * F)
            w2_in.append(load(f"w2_{g}", w_stage[:, 1, cols].rearrange("p (m d) -> p m d", d=D),
                              w2[g * ep:(g + 1) * ep].rearrange("e (j p) d -> p (e j) d", p=P)))
        b2_in = load("b2", b2_sb[:, :], b2.rearrange("(o e) d -> o (e d)", o=1).broadcast_to([P, E * D]))
        proj_in = load("w_proj", w_proj32[:, :], w_proj)
        wo_in = load("w_o", w_o_sb[:, :, :], w_o.rearrange("(k p) d -> p k d", p=P))
        gnorm_in = load("gnorm", gnorm_sb[:, :], gnorm)
        rope_in = load("rope", rope_sb[:, :], rope)

        rs_val, rs_tmp, rs_out = sb("rs_val", [P, NT]), sb("rs_tmp", [P, NT]), sb("rs_out", [P, NT])
        rs_int = sb("rs_int", [P, NT], I32)

        def rsqrt_steps(n, ready, out_read):
            v, t, y, i = rs_val[:, 0:n], rs_tmp[:, 0:n], rs_out[:, 0:n], rs_int[:, 0:n]
            dve.wait(ready)
            m = dve.mark(dve.engine.tensor_scalar(i, v.bitcast(I32), 1, None, ALU.logical_shift_right))
            yield m
            dve.wait(m, *out_read)
            m = dve.mark(dve.engine.tensor_scalar(y.bitcast(I32), i, -1.0, RSQRT_MAGIC, ALU.mult, ALU.add))
            yield m
            for _ in range(NEWTON_STEPS):
                dve.wait(m)
                m = dve.mark(dve.engine.tensor_tensor(t, y, v, ALU.mult))
                yield m
                dve.wait(m)
                m = dve.mark(dve.engine.scalar_tensor_tensor(t, t, -0.5, y, ALU.mult, ALU.mult))
                yield m
                dve.wait(m)
                m = dve.mark(dve.engine.scalar_tensor_tensor(y, t, 1.5, y, ALU.add, ALU.mult))
                yield m

        gate_sq = sb("gate_sq", [E, GATE])
        gate_ss = sb("gate_ss", [E, 1])
        gate_wn = sb("gate_wn", [E, GATE])
        gate_wnT = sb("gate_wnT", [GATE, E])
        gate_w32 = sb("gate_w32", [P, E])
        gate_w16 = sb("gate_w16", [P, 2, E], F16)

        COL_GATE = NT // LOADS

        def gate_norms():
            ones = dve.mark(dve.engine.memset(rs_val[:, :], 1.0))
            dve.wait(wg_in)
            m = dve.mark(dve.engine.tensor_tensor(gate_sq[:, :], wg_sb[:, :], wg_sb[:, :], ALU.mult))
            dve.wait(m)
            m = dve.mark(dve.engine.tensor_reduce(gate_ss[:, :], gate_sq[:, :], AX.X, ALU.add))
            dve.wait(m, ones)
            return dve.mark(dve.engine.tensor_scalar(rs_val[0:E, COL_GATE:COL_GATE + 1], gate_ss[:, :], 1e-8, None, ALU.max))

        def gate_weights(rs_ready):
            dve.wait(rs_ready)
            scaled = dve.mark(dve.engine.tensor_scalar(gate_wn[:, :], wg_sb[:, :], rs_out[0:E, COL_GATE:COL_GATE + 1], None, ALU.mult))
            pe.wait(scaled, masks_in)
            bank = banks[7]
            m = pe.mark(pe.engine.transpose(bank[0:GATE, 0:E], gate_wn[:, :], ident32[0:E, 0:E]))
            act.wait(m)
            m = act.mark(act.engine.activation(gate_wnT[:, :], bank[0:GATE, 0:E], ACT.Copy))
            emptied[7] = m
            pe.wait(m, w_redT_in)
            bank = banks[6]
            m = pe.mark(pe.engine.matmul(bank[:, 0:E], w_redT_sb[:, :], gate_wnT[:, :], start=True, stop=True))
            act.wait(m)
            m = act.mark(act.engine.activation(gate_w32[:, :], bank[:, 0:E], ACT.Copy, scale=WEIGHT_SCALE))
            emptied[6] = m
            act.wait(m)
            m = act.mark(act.engine.activation(gate_w16[:, 0, :], gate_w32[:, :], ACT.Copy))
            pool.wait(m)
            return pool.mark(pool.engine.tensor_tensor(gate_w16[:, 1, :], gate_w32[:, :], gate_w16[:, 0, :], ALU.subtract)), scaled

        def weights_hi(hi, src, loaded):
            act.wait(loaded)
            scaled = act.mark(act.engine.activation(src, src, ACT.Copy, scale=WEIGHT_SCALE))
            act.wait(scaled)
            return act.mark(act.engine.activation(hi, src, ACT.Copy))

        def weights_lo(lo, src, hi, hi_ready):
            pool.wait(hi_ready)
            return pool.mark(pool.engine.tensor_tensor(lo, src, hi, ALU.subtract))

        def expert_weights_views(w16, which, g):
            src = w_stage[:, which, g * ep * F:(g + 1) * ep * F].rearrange("p (m c) -> p m c", c=P)
            dst = w16[:, g * ep * 2 * F:(g + 1) * ep * 2 * F].rearrange("p (m h c) -> p m h c", h=2, c=P)
            return src, dst[:, :, 0, :], dst[:, :, 1, :]

        def expert_weights_hi(w16, which, g, loaded):
            src, hi, lo = expert_weights_views(w16, which, g)
            return weights_hi(hi, src, loaded)

        def expert_weights_lo(w16, which, g, hi_ready):
            src, hi, lo = expert_weights_views(w16, which, g)
            return weights_lo(lo, src, hi, hi_ready)

        def split_expert_weights(w16, which, g, loaded):
            return expert_weights_lo(w16, which, g, expert_weights_hi(w16, which, g, loaded))

        def layernorm_stats(tiles, ready):
            marks = []
            for t, m in zip(tiles, ready):
                dve.wait(m)
                marks.append(dve.mark(dve.engine.bn_stats(row_stats[:, t, :], x_sb[:, t, :])))
            for t, m in zip(tiles, marks):
                dve.wait(m)
                m = dve.mark(dve.engine.bn_aggr(row_mean_var[:, t, :], row_stats[:, t, :]))
            return m

        def layernorm_value(col, t0, n, stats_ready, val_read):
            k = ROW_SCALE ** -2
            dve.wait(stats_ready, val_read)
            return dve.mark(dve.engine.tensor_scalar(rs_val[:, col:col + n], row_mean_var[:, t0:t0 + n, 1],
                                                     k, EPS * k, ALU.mult, ALU.add))

        ROW_BUFS = SEQS
        xn32 = ring("xn32_", ROW_BUFS, [P, TPS, D])
        xn16 = ring("xn16_", ROW_BUFS, [P, TPS, 2, D], F16)
        rows_store = dma_counters("rows_stored", ROW_BUFS)
        xn32_read = [None] * ROW_BUFS
        xn16_transposed = [None] * ROW_BUFS
        xn16_stored = [None] * ROW_BUFS

        def normalise(seq, buf, col, rs_ready):
            n32 = xn32[buf]
            dve.wait(rs_ready, xn32_read[buf])
            for j in range(TPS):
                t = TPS * seq + j
                m = dve.mark(dve.engine.tensor_scalar(n32[:, j, :], x_sb[:, t, :], row_mean_var[:, t, 0:1],
                                                      rs_out[:, col + j:col + j + 1], ALU.subtract, ALU.mult))
            return m

        def rows_hi(buf, normalised):
            act.wait(normalised, xn16_transposed[buf], xn16_stored[buf])
            return act.mark(act.engine.activation(xn16[buf][:, :, 0, :], xn32[buf][:, :, :], ACT.Copy))

        def rows_lo(buf, hi, lo_engine):
            n32, n16 = xn32[buf], xn16[buf]
            lo_engine.wait(hi)
            lo = lo_engine.mark(lo_engine.engine.tensor_tensor(n16[:, :, 1, :], n32[:, :, :], n16[:, :, 0, :], ALU.subtract))
            xn32_read[buf] = lo
            return lo

        def store_rows(k, seq, buf, split):
            sp.wait_ge(*split)
            rows = rows_dram[k].ap().rearrange("(t p) c -> p t c", p=P)[:, TPS * seq:TPS * (seq + 1), :]
            xn16_stored[buf] = rows_store[buf].mark(
                sp.dma_start(rows, xn16[buf][:, :, :, :].rearrange("p t h d -> p t (h d)")))
            return xn16_stored[buf]

        xnT_read = [None] * SEQS

        def transpose_rows(seq, buf, split, b):
            n16 = xn16[buf]
            b16 = banks[b][:, :].bitcast(F16)
            pe.wait(split, halves_in, emptied[b])
            for h in range(2):
                for j in range(TPS):
                    c = (h * TPS + j) * P
                    m = pe.engine.transpose(b16[:, c:c + P], n16[:, j, h, :], ident16)
            m = pe.mark(m)
            xn16_transposed[buf] = m
            act.wait(m, xnT_read[seq])
            m = act.mark(act.engine.activation(xnT[:, :, seq * T:(seq + 1) * T],
                                               b16[:, 0:2 * T].rearrange("p (h t) -> p h t", h=2), ACT.Copy))
            emptied[b] = m
            return m

        logits = sb("logits", [P, NT, E])

        def gate_logits(seq, xT_ready, w_ready, b, logits_read):
            bank = banks[b]
            pe.wait(xT_ready, w_ready, emptied[b])
            for j in range(TPS):
                t = TPS * seq + j
                hi, lo = xnT[:, 0, t * P:(t + 1) * P], xnT[:, 1, t * P:(t + 1) * P]
                o = bank[:, j * E:(j + 1) * E]
                pe.engine.matmul(o, hi, gate_w16[:, 0, :], start=True, stop=False)
                pe.engine.matmul(o, hi, gate_w16[:, 1, :], start=False, stop=False)
                m = pe.engine.matmul(o, lo, gate_w16[:, 0, :], start=False, stop=True)
            m = pe.mark(m)
            xnT_read[seq] = m
            act.wait(m, logits_read)
            m = act.mark(act.engine.activation(logits[:, TPS * seq:TPS * (seq + 1), :],
                                               bank[:, 0:TPS * E].rearrange("p (t e) -> p t e", e=E),
                                               ACT.Copy, scale=UNSCALE))
            emptied[b] = m
            return m

        shape_te = [P, NT, E]
        r_max = sb("r_max", [P, NT])
        r_shift = sb("r_shift", shape_te)
        r_exp = sb("r_exp", shape_te)
        r_sum = sb("r_sum", [P, NT])
        half_score = [sb(f"half_score{k}", [P, NT]) for k in range(2)]
        r_cand = sb("r_cand", shape_te)
        r_expert = sb("r_expert", [P, NT])
        member = sb("member", shape_te, F16)
        count16 = sb("count16", [P, P], F16)
        r_rank = sb("r_rank", shape_te)
        r_total = sb("r_total", [P, E])
        r_cmp = sb("r_cmp", [P, E, NT])
        r_tiles = sb("r_tiles", [P, E])
        r_tri = sb("r_tri", [P, E, E])
        r_start = sb("r_start", [P, E])
        r_start_slot = sb("r_start_slot", [P, E])
        r_posf = sb("r_posf", [P, NT])
        slot_of = [sb(f"slot_of{k}", [P, NT], U32) for k in range(2)]
        r_posi = sb("r_posi", [P, NT], I32)
        r_rowi = sb("r_rowi", [P, NT], I32)
        r_tilei = sb("r_tilei", [P, NT], I32)
        r_rowf = sb("r_rowf", [P, NT])
        r_tilef = sb("r_tilef", [P, NT])
        row_hot = sb("row_hot", [P, NT, P], F16)
        tile_hot = sb("tile_hot", [P, NT, NS])
        tile_token = sb("tile_token", [P, NT, NS], F16)
        token_of = [sb(f"token_of{k}", [P, NS], U32) for k in range(2)]
        s_cmp = sb("s_cmp", [1, NS, E - 1])
        s_expert = sb("s_expert", [1, NS])
        offsets = [sb(f"offsets{k}", [1, 3, NS], I32) for k in range(2)]
        OFF_W, OFF_B1, OFF_B2 = range(3)

        def route(k, logits_ready):
            v = dve.engine

            def step(instruction):
                m = dve.mark(instruction)
                dve.wait(m)
                return m

            def over_experts(a):
                return a.unsqueeze(2).broadcast_to(shape_te)

            dve.wait(logits_ready, consts_in)
            step(v.tensor_reduce(r_max[:, :], logits[:, :, :], AX.X, ALU.max))
            shifted = step(v.tensor_tensor(r_shift[:, :, :], logits[:, :, :], over_experts(r_max[:, :]), ALU.subtract))
            act.wait(shifted)
            exps = act.mark(act.engine.activation(r_exp[:, :, :], r_shift[:, :, :], ACT.Exp))
            iota_e = c32[:, C_IOTA_E:C_IOTA_S].unsqueeze(1).broadcast_to(shape_te)
            step(v.tensor_scalar(r_cand[:, :, :], r_shift[:, :, :], 0.0, float(E), ALU.is_lt, ALU.mult))
            step(v.tensor_tensor(r_cand[:, :, :], r_cand[:, :, :], iota_e, ALU.add))
            step(v.tensor_reduce(r_expert[:, :], r_cand[:, :, :], AX.X, ALU.min))
            m = step(v.tensor_tensor(member[:, :, :], iota_e, over_experts(r_expert[:, :]), ALU.is_equal))
            members = member[:, :, :].rearrange("p t e -> p (t e)")
            counts, ranks, tokens = banks[0], banks[1], banks[2]
            pe.wait(m, emptied[0])
            m = pe.mark(pe.engine.matmul(counts[:, 0:P], members, ones16, start=True, stop=True))
            dve.wait(m)
            m = dve.mark(v.tensor_copy(count16[:, :], counts[:, 0:P]))
            emptied[0] = m
            pe.wait(m, emptied[1])
            pe.engine.matmul(ranks[:, P:P + E], count16[:, :], expert16, start=True, stop=True)
            pe.engine.matmul(ranks[:, 0:P], before16, members, start=True, stop=False)
            ranked = pe.mark(pe.engine.matmul(ranks[:, 0:P], count16[:, :], tile_before16, start=False, stop=True))
            dve.wait(ranked)
            step(v.tensor_copy(r_total[:, :], ranks[:, P:P + E]))
            thresholds = c32[:, C_THRESH:C_IOTA_E].unsqueeze(1).broadcast_to([P, E, NT])
            step(v.tensor_tensor(r_cmp[:, :, :], r_total[:, :].unsqueeze(2).broadcast_to([P, E, NT]), thresholds, ALU.is_gt))
            step(v.tensor_reduce(r_tiles[:, :], r_cmp[:, :, :], AX.X, ALU.add))
            before = c32[:, C_BEFORE:C_TOKEN].rearrange("p (a b) -> p a b", a=E)
            step(v.tensor_tensor(r_tri[:, :, :], r_tiles[:, :].unsqueeze(1).broadcast_to([P, E, E]), before, ALU.mult))
            started = step(v.tensor_reduce(r_start[:, :], r_tri[:, :, :], AX.X, ALU.add))
            step(v.tensor_scalar(r_start_slot[:, :], r_start[:, :], float(P), None, ALU.mult))
            m = step(v.tensor_tensor(r_rank[:, :, :], ranks[:, 0:P].rearrange("p (t e) -> p t e", e=E),
                                     r_start_slot[:, :].unsqueeze(1).broadcast_to(shape_te), ALU.add))
            emptied[1] = m
            step(v.tensor_tensor(r_rank[:, :, :], r_rank[:, :, :], member[:, :, :], ALU.mult))
            step(v.tensor_reduce(r_posf[:, :], r_rank[:, :, :], AX.X, ALU.add))
            step(v.tensor_copy(r_posi[:, :], r_posf[:, :]))
            dve.mark(v.tensor_scalar(r_rowi[:, :], r_posi[:, :], P - 1, None, ALU.bitwise_and))
            split_pos = dve.mark(v.tensor_scalar(r_tilei[:, :], r_posi[:, :], 7, None, ALU.logical_shift_right))
            iota_s = c32[0:1, C_IOTA_S:C_BEFORE].unsqueeze(2).broadcast_to([1, NS, E - 1])
            starts = r_start[0:1, 1:E].unsqueeze(1).broadcast_to([1, NS, E - 1])
            dve.wait(started)
            compared = dve.mark(v.tensor_tensor(s_cmp[:, :, :], starts, iota_s, ALU.is_le))
            dve.wait(split_pos)
            dve.mark(v.tensor_copy(r_rowf[:, :], r_rowi[:, :]))
            located = dve.mark(v.tensor_copy(r_tilef[:, :], r_tilei[:, :]))
            dve.wait(compared)
            experts_known = dve.mark(v.tensor_reduce(s_expert[:, :], s_cmp[:, :, :], AX.X, ALU.add))
            shape_ts = [P, NT, NS]
            iota_ts = c32[:, C_IOTA_S:C_BEFORE].unsqueeze(1).broadcast_to(shape_ts)
            dve.wait(located)
            hot = dve.mark(v.tensor_tensor(tile_hot[:, :, :], iota_ts, r_tilef[:, :].unsqueeze(2).broadcast_to(shape_ts), ALU.is_equal))
            dve.wait(experts_known)
            for row, unit in ((OFF_W, 2 * F), (OFF_B1, NF), (OFF_B2, D)):
                offsets_ready = dve.mark(v.tensor_scalar(offsets[k][:, row, :], s_expert[:, :], float(unit), None, ALU.mult))
            dve.wait(hot)
            dve.mark(v.tensor_tensor(tile_token[:, :, :], tile_hot[:, :, :],
                                     c32[:, C_TOKEN:C_COLS].unsqueeze(2).broadcast_to(shape_ts), ALU.mult))
            pe.wait(emptied[2])
            for t in range(NT):
                m = dve.mark(v.tensor_scalar(row_hot[:, t, :], iota16, r_rowf[:, t:t + 1], None, ALU.is_equal))
                pe.wait(m)
                m = pe.engine.matmul(tokens[:, 0:NS], row_hot[:, t, :], tile_token[:, t, :], start=(t == 0), stop=(t == NT - 1))
            m = pe.mark(m)
            slots_ready = dve.mark(v.tensor_copy(slot_of[k][:, :], r_posf[:, :]))
            dve.wait(m)
            tokens_ready = dve.mark(v.tensor_copy(token_of[k][:, :], tokens[:, 0:NS]))
            emptied[2] = tokens_ready
            dve.wait(exps)
            step(v.tensor_reduce(r_sum[:, :], r_exp[:, :, :], AX.X, ALU.add))
            step(v.reciprocal(half_score[k][:, :], r_sum[:, :]))
            scores_ready = dve.mark(v.tensor_scalar(half_score[k][:, :], half_score[k][:, :], 0.5, None, ALU.mult))
            return slots_ready, scores_ready, tokens_ready, offsets_ready

        GATHERS, SLOTS_T, HIDDEN, RESULTS = 8, 3, 3, 4
        slot_rows = ring("slot_rows", GATHERS, [P, 2, D], F16)
        gather_done = dma_counters("gathered", GATHERS)
        slotT = ring("slotT", SLOTS_T, [P, 2, P], F16)
        hidden32 = ring("hidden32_", HIDDEN, [P, NF, P])
        hidden16 = ring("hidden16_", HIDDEN, [P, 2, NF, P], F16)
        y_sb = ring("y_sb", RESULTS, [P, D])
        y_store = dma_counters("y_stored", RESULTS)
        BANK_T, BANK_UP, BANK_DOWN = (0, 1, 7), (2, 3, 4), (5, 6)
        gathered, transposed, t_copied, up_done, activated, hidden_split, down_done, y_stored = ({} for _ in range(8))

        def load_offsets(eng, k, row, limit, ready):
            regs = [eng.engine.alloc_register(f"off{k}_{row}_{i}") for i in range(NS)]
            eng.wait(ready)
            eng.engine.reg_load(regs, offsets[k][0:1, row, :])
            return [eng.engine.snap(r, min_val=0, max_val=limit) for r in regs]

        def experts(k, rows_stored, tokens_ready, offsets_ready, w1_ready, last_of_w2=None):
            s0, s1 = k * NS, (k + 1) * NS
            w_off = load_offsets(pe, k, OFF_W, (E - 1) * 2 * F, offsets_ready)
            b1_off = load_offsets(act, k, OFF_B1, (E - 1) * NF, offsets_ready)
            b2_off = load_offsets(dve, k, OFF_B2, (E - 1) * D, offsets_ready)
            pool.wait(tokens_ready, *rows_stored)
            pe.wait(w1_ready, *(emptied[b] for b in BANK_T + BANK_UP + BANK_DOWN))
            act.wait(b1_in)
            dve.wait(b2_in)

            def gather(s):
                pool.wait(transposed.get(s - GATHERS))
                gathered[s] = gather_done[s % GATHERS].mark(pool.engine.indirect_dma_start(
                    slot_rows[s % GATHERS][:, :, :].rearrange("p h d -> p (h d)"), None, rows_dram[k].ap(),
                    bass.IndirectOffsetOnAxis(token_of[k][:, s - s0:s - s0 + 1], 0)))

            def transpose(s):
                rows, t16 = slot_rows[s % GATHERS], slotT[s % SLOTS_T]
                b = BANK_T[s % len(BANK_T)]
                b16 = banks[b][:, :].bitcast(F16)
                pe.wait(gathered[s])
                pe.engine.transpose(b16[:, 0:P], rows[:, 0, :], ident16)
                transposed[s] = pe.mark(pe.engine.transpose(b16[:, P:2 * P], rows[:, 1, :], ident16))
                act.wait(transposed[s], up_done.get(s - SLOTS_T))
                t_copied[s] = act.mark(act.engine.activation(t16[:, :, :], b16[:, 0:2 * P].rearrange("p (h t) -> p h t", h=2), ACT.Copy))
                emptied[b] = t_copied[s]

            def up(s):
                hi, lo = slotT[s % SLOTS_T][:, 0, :], slotT[s % SLOTS_T][:, 1, :]
                b = BANK_UP[s % len(BANK_UP)]
                pe.wait(t_copied[s])
                for f in range(NF):
                    o = banks[b][:, f * P:(f + 1) * P]
                    w_hi, w_lo = (w1_16[:, bass.ds(w_off[s - s0] + (2 * f + part) * P, P)] for part in range(2))
                    pe.engine.matmul(o, w_hi, hi, start=True, stop=False)
                    pe.engine.matmul(o, w_hi, lo, start=False, stop=False)
                    m = pe.engine.matmul(o, w_lo, hi, start=False, stop=True)
                up_done[s] = pe.mark(m)

            def activate(s):
                h = hidden32[s % HIDDEN]
                b = BANK_UP[s % len(BANK_UP)]
                act.wait(up_done[s], hidden_split.get(s - HIDDEN))
                bias = b1_sb[:, bass.ds(b1_off[s - s0], NF)]
                for f in range(NF):
                    m = act.mark(act.engine.activation(h[:, f, :], banks[b][:, f * P:(f + 1) * P], ACT.Gelu,
                                                       bias=bias[:, f:f + 1], scale=UNSCALE))
                activated[s] = emptied[b] = m

            def split(s):
                h, parts = hidden32[s % HIDDEN], hidden16[s % HIDDEN]
                dve.wait(activated[s], down_done.get(s - HIDDEN))
                m = dve.mark(dve.engine.tensor_copy(parts[:, 0, :, :], h[:, :, :]))
                dve.wait(m)
                hidden_split[s] = dve.mark(dve.engine.tensor_tensor(parts[:, 1, :, :], h[:, :, :], parts[:, 0, :, :], ALU.subtract))

            def down(s):
                parts = hidden16[s % HIDDEN]
                b = BANK_DOWN[s % len(BANK_DOWN)]
                pe.wait(hidden_split[s])
                for f in range(NF):
                    w = w2_16[:, bass.ds(w_off[s - s0] + 2 * f * D, 2 * D)]
                    if f == 0:
                        pe.engine.matmul(banks[b][:, 0:2 * D], parts[:, 0, f, :], w, start=True, stop=False)
                    pe.engine.matmul(banks[b][:, 0:D], parts[:, 1, f, :], w[:, 0:D], start=False, stop=False)
                    if f > 0:
                        m = pe.engine.matmul(banks[b][:, 0:2 * D], parts[:, 0, f, :], w, start=False, stop=(f == NF - 1))
                down_done[s] = pe.mark(m)

            def finish(s):
                y = y_sb[s % RESULTS]
                b = BANK_DOWN[s % len(BANK_DOWN)]
                dve.wait(down_done[s], y_stored.get(s - RESULTS))
                m = dve.mark(dve.engine.scalar_tensor_tensor(y[:, :], banks[b][:, 0:D], 1.0 / WEIGHT_SCALE,
                                                             b2_sb[:, bass.ds(b2_off[s - s0], D)], ALU.mult, ALU.add))
                dve.wait(m)
                m = dve.mark(dve.engine.scalar_tensor_tensor(y[:, :], banks[b][:, D:2 * D], 1.0 / WEIGHT_SCALE,
                                                             y[:, :], ALU.mult, ALU.add))
                emptied[b] = m
                sp.wait_ge(*m)
                y_stored[s] = y_store[s % RESULTS].mark(sp.dma_start(y_dram[k].ap()[(s - s0) * P:(s - s0 + 1) * P, :], y[:, :]))

            T_AHEAD = SLOTS_T - 1
            for s in range(s0, s0 + GATHERS // 2):
                gather(s)
            w2_ready = last_of_w2() if last_of_w2 is not None else None
            for s in range(s0 + GATHERS // 2, s0 + GATHERS - 1):
                gather(s)
            for s in range(s0, s0 + T_AHEAD):
                transpose(s)
            for s in range(s0, s1 + 2):
                if s + GATHERS - 1 < s1:
                    gather(s + GATHERS - 1)
                if s + T_AHEAD < s1:
                    transpose(s + T_AHEAD)
                if s < s1:
                    up(s)
                    activate(s)
                if s == s0:
                    pe.wait(w2_ready)
                if s0 <= s - 2:
                    down(s - 2)
                if s0 <= s - 1 < s1:
                    split(s - 1)
                if s0 <= s - 2:
                    finish(s - 2)
            return [y_stored[s] for s in range(s1 - RESULTS, s1)]

        BACK = 6
        back = ring("back", BACK, [P, D])
        back_landed = dma_counters("back_landed", BACK)
        fetched, added_back = {}, {}

        def fetch(k, t):
            n = k * NT + t
            pool.wait(added_back.get(n - BACK))
            fetched[n] = back_landed[n % BACK].mark(pool.engine.indirect_dma_start(
                back[n % BACK][:, :], None, y_dram[k].ap(), bass.IndirectOffsetOnAxis(slot_of[k][:, t:t + 1], 0)))

        def add_back(k, t, x_ready=None):
            n = k * NT + t
            dve.wait(fetched[n], x_ready)
            added_back[n] = dve.mark(dve.engine.scalar_tensor_tensor(x_sb[:, t, :], back[n % BACK][:, :], half_score[k][:, t:t + 1],
                                                                     x_sb[:, t, :], ALU.mult, ALU.add))
            return added_back[n]

        rows_stored = []
        group = NT // LOADS
        seqs = group // TPS
        gate_value = gate_norms()
        rs_free = None
        for g in range(LOADS):
            tiles = range(g * group, (g + 1) * group)
            m = layernorm_stats(tiles, [x_in[g]] + [None] * (group - 1))
            m = layernorm_value(0, g * group, group, m, rs_free)
            dve.wait(gate_value if g == 0 else None)
            *_, rs_ready = rsqrt_steps(group + (g == 0), m, [rs_free])
            span = range(g * seqs, (g + 1) * seqs)
            hi, split, xT = {}, {}, {}
            for seq in span:
                normalised = normalise(seq, seq % ROW_BUFS, TPS * seq - g * group, rs_ready)
                hi[seq] = rows_hi(seq % ROW_BUFS, normalised)
            if g == 0:
                gate_ready, _ = gate_weights(rs_ready)
            for seq in span:
                split[seq] = rows_lo(seq % ROW_BUFS, hi[seq], dve)
                rs_free = split[seq]
                rows_stored.append(store_rows(0, seq, seq % ROW_BUFS, split[seq]))
                xT[seq] = transpose_rows(seq, seq % ROW_BUFS, split[seq], seq % 4)
            for seq in span:
                logits_ready = gate_logits(seq, xT[seq], gate_ready, 4 + seq % 4, None)
            if g == 0:
                for part in range(W_PARTS // 2):
                    w1_ready = split_expert_weights(w1_16, 0, part, w1_in[part])
        for part in range(W_PARTS // 2, W_PARTS):
            w1_ready = split_expert_weights(w1_16, 0, part, w1_in[part])
        for part in range(W_PARTS - 1):
            split_expert_weights(w2_16, 1, part, w2_in[part])
        slots_ready, scores_ready, tokens_ready, offsets_ready = route(0, logits_ready)
        w2_last = expert_weights_hi(w2_16, 1, W_PARTS - 1, w2_in[W_PARTS - 1])
        proj_hi = weights_hi(w_proj16[:, 0, :], w_proj32[:, :], proj_in)
        results_stored = experts(0, rows_stored, tokens_ready, offsets_ready, w1_ready,
                                 lambda: expert_weights_lo(w2_16, 1, W_PARTS - 1, w2_last))

        proj_ready = weights_lo(w_proj16[:, 1, :], w_proj32[:, :], w_proj16[:, 0, :], proj_hi)
        pool.wait(wo_in, gnorm_in)
        wo_ready = pool.mark(pool.engine.tensor_scalar(w_o_sb[:, :, :], w_o_sb[:, :, :], gnorm_sb[:, 0:1], None, ALU.mult))

        CHUNKS = VD // P
        rot_tmp = ring("rot_tmp", 2, [P, 2, 2 * T])
        rotated = ring("rotated", 2, [P, 2 * T])
        values = ring("values", 3, [P, TPS, VD])
        silu_gT = ring("silu_gT", 3, [P, CHUNKS, T])
        weights = ring("weights", 2, [P, HEADS, 3 * P])
        squaresT = sb("squaresT", [P, CHUNKS, T])
        gatedT = ring("gatedT", 2, [P, CHUNKS, T])
        norm_bias = sb("norm_bias", [P, 2 * TPS])
        BANK_OUT, BANK_ROWS, BANK_MIX = (0, 1), 2, 7
        BANK_QK, BANK_V, BANK_G = (3, 4), 5, 6
        BANK_SCORE = (3, 4, 5, 6)
        COL_X1, COL_X2, COL_HEAD = 0, TPS, 2 * TPS
        RS_N = COL_HEAD + TPS * HEADS
        (norm1, norm2, split1, split2, xT_ready, qk_done, rot_ready, v_ready, g_ready, scored, masked, mixed,
         squared, heads_gated, projected_out, sums_done, sums_ready, attended) = ({} for _ in range(18))

        def add_first(b):
            tiles = [TPS * b + j for j in range(TPS)]
            added, stats = {}, {}

            def add(t):
                added[t] = add_back(0, t)

            def stat(t):
                dve.wait(added[t])
                stats[t] = dve.mark(dve.engine.bn_stats(row_stats[:, t, :], x_sb[:, t, :]))

            def aggregate(t):
                dve.wait(stats[t])
                stats[t] = dve.mark(dve.engine.bn_aggr(row_mean_var[:, t, :], row_stats[:, t, :]))

            return [lambda t=t, f=f: f(t) for f in (add, stat, aggregate) for t in tiles], lambda: stats[tiles[-1]]

        def normalise_on_act(b, buf, col, rs_ready, bias_read):
            bias = norm_bias[:, col:col + TPS]
            mean = row_mean_var[:, TPS * b:TPS * (b + 1), 0]
            dve.wait(rs_ready, bias_read)
            m = dve.mark(dve.engine.scalar_tensor_tensor(bias, mean, -1.0, rs_out[:, col:col + TPS], ALU.mult, ALU.mult))
            act.wait(m, xn32_read[buf])
            for j in range(TPS):
                m = act.mark(act.engine.activation(xn32[buf][:, j, :], x_sb[:, TPS * b + j, :], ACT.Identity,
                                                   bias=norm_bias[:, col + j:col + j + 1], scale=rs_out[:, col + j:col + j + 1]))
            return m

        def project_qk(b):
            span = slice(b * T, (b + 1) * T)
            hi, lo = xnT[:, 0, span], xnT[:, 1, span]
            pe.wait(xT_ready[b])
            for swapped in range(2):
                bank = banks[BANK_QK[swapped]]
                pe.wait(emptied[BANK_QK[swapped]])
                for j in range(2):
                    c = (2 * j + swapped) * P
                    w_hi, w_lo = w_proj16[:, 0, c:c + P], w_proj16[:, 1, c:c + P]
                    o = bank[:, j * T:(j + 1) * T]
                    pe.engine.matmul(o, w_hi, hi, start=True, stop=False)
                    pe.engine.matmul(o, w_hi, lo, start=False, stop=False)
                    m = pe.engine.matmul(o, w_lo, hi, start=False, stop=True)
                qk_done[b, swapped] = pe.mark(m)

        def rotate(b):
            tmp, r = rot_tmp[b % 2], rotated[b % 2]
            dve.wait(rot_ready.get(b - 2))
            for j in range(2):
                dve.wait(qk_done[b, j])
                m = dve.mark(dve.engine.tensor_tensor(tmp[:, j, :], banks[BANK_QK[j]][:, :], rope_sb[:, j * 2 * T:(j + 1) * 2 * T], ALU.mult))
                emptied[BANK_QK[j]] = m
            pool.wait(m, scored.get(b - 2))
            rot_ready[b] = pool.mark(pool.engine.tensor_tensor(r[:, :], tmp[:, 0, :], tmp[:, 1, :], ALU.add))

        def project_vg(b):
            span = slice(b * T, (b + 1) * T)
            x_hi, x_lo = xnT[:, 0, span], xnT[:, 1, span]
            v_hi, v_lo = w_proj16[:, 0, 4 * P:4 * P + VD], w_proj16[:, 1, 4 * P:4 * P + VD]
            pe.wait(emptied[BANK_V])
            for j in range(TPS):
                hi, lo = x_hi[:, j * P:(j + 1) * P], x_lo[:, j * P:(j + 1) * P]
                o = banks[BANK_V][:, j * VD:(j + 1) * VD]
                pe.engine.matmul(o, hi, v_hi, start=True, stop=False)
                pe.engine.matmul(o, hi, v_lo, start=False, stop=False)
                m = pe.engine.matmul(o, lo, v_hi, start=False, stop=True)
            m = pe.mark(m)
            act.wait(m, mixed.get(b - 3))
            v_ready[b] = act.mark(act.engine.activation(values[b % 3][:, :, :].rearrange("p t c -> p (t c)"),
                                                        banks[BANK_V][:, :], ACT.Copy, scale=UNSCALE))
            emptied[BANK_V] = v_ready[b]
            pe.wait(emptied[BANK_G])
            for c in range(CHUNKS):
                cols = slice(4 * P + VD + c * P, 4 * P + VD + (c + 1) * P)
                w_hi, w_lo = w_proj16[:, 0, cols], w_proj16[:, 1, cols]
                o = banks[BANK_G][:, c * T:(c + 1) * T]
                pe.engine.matmul(o, w_hi, x_hi, start=True, stop=False)
                pe.engine.matmul(o, w_hi, x_lo, start=False, stop=False)
                m = pe.engine.matmul(o, w_lo, x_hi, start=False, stop=True)
            m = pe.mark(m)
            xnT_read[b] = m
            act.wait(m, heads_gated.get(b - 3))
            g_ready[b] = act.mark(act.engine.activation(silu_gT[b % 3][:, :, :].rearrange("p c t -> p (c t)"),
                                                        banks[BANK_G][:, :], ACT.Silu, scale=UNSCALE))
            emptied[BANK_G] = g_ready[b]

        def score(b):
            r = rotated[b % 2]
            pe.wait(rot_ready[b])
            for h in range(HEADS):
                hs = slice(h * DK, (h + 1) * DK)
                pe.wait(emptied[BANK_SCORE[h]])
                pe.engine.matmul(banks[BANK_SCORE[h]][:, 0:2 * P], r[hs, T:T + P], r[hs, 0:T], start=True, stop=True,
                                 tile_position=(h * DK, 0))
            for h in range(HEADS):
                hs = slice(h * DK, (h + 1) * DK)
                scored[b, h] = pe.mark(pe.engine.matmul(banks[BANK_SCORE[h]][:, 2 * P:3 * P], r[hs, T + P:2 * T], r[hs, P:T],
                                                        start=True, stop=True, tile_position=(h * DK, 0)))
            scored[b] = scored[b, HEADS - 1]

        def mask(b):

            def head(h):
                dve.wait(scored[b, h], mixed.get(b - 2) if h == 0 else None)
                m = dve.mark(dve.engine.tensor_tensor(weights[b % 2][:, h, :], banks[BANK_SCORE[h]][:, 0:3 * P], score_mask, ALU.mult))
                emptied[BANK_SCORE[h]] = masked[b] = m

            return [lambda h=h: head(h) for h in range(HEADS)]

        def mix(b):
            w, v, bank = weights[b % 2], values[b % 3], banks[BANK_MIX]
            pe.wait(masked[b], v_ready[b], emptied[BANK_MIX])
            for h in range(HEADS):
                c, r = divmod(h, P // DV)
                rows, cols = slice(r * DV, (r + 1) * DV), slice(h * DV, (h + 1) * DV)
                at = (0, r * DV)
                q0, q1 = bank[rows, c * T:c * T + P], bank[rows, c * T + P:(c + 1) * T]
                pe.engine.matmul(q0, v[:, 0, cols], w[:, h, 0:P], start=True, stop=True, tile_position=at)
                pe.engine.matmul(q1, v[:, 0, cols], w[:, h, P:2 * P], start=True, stop=False, tile_position=at)
                m = pe.engine.matmul(q1, v[:, 1, cols], w[:, h, 2 * P:3 * P], start=False, stop=True, tile_position=at)
            mixed[b] = pe.mark(m)

        def square_heads(b):
            bank = banks[BANK_MIX]
            act.wait(mixed[b], sums_done.get(b - 1))
            squared[b] = act.mark(act.engine.activation(squaresT[:, :, :].rearrange("p c t -> p (c t)"), bank[:, :], ACT.Square))

        def gate_heads(b):
            dve.wait(squared[b], g_ready[b], projected_out.get(b - 2))
            m = dve.mark(dve.engine.tensor_tensor(gatedT[b % 2][:, :, :].rearrange("p c t -> p (c t)"), banks[BANK_MIX][:, :],
                                                  silu_gT[b % 3][:, :, :].rearrange("p c t -> p (c t)"), ALU.mult))
            heads_gated[b] = emptied[BANK_MIX] = m

        def sum_heads(b, val_read):
            bank = banks[BANK_ROWS]
            pe.wait(squared[b], emptied[BANK_ROWS])
            per = P // DV
            for j in range(TPS):
                for c in range(CHUNKS):
                    o = bank[:, j * HEADS + c * per:j * HEADS + (c + 1) * per]
                    m = pe.engine.matmul(o, squaresT[:, c, j * P:(j + 1) * P], head_rows, start=True, stop=True)
            sums_done[b] = pe.mark(m)
            act.wait(sums_done[b], val_read)
            sums_ready[b] = act.mark(act.engine.activation(rs_val[:, COL_HEAD:RS_N], bank[:, 0:TPS * HEADS], ACT.Copy,
                                                           bias=EPS, scale=1.0 / DV))
            emptied[BANK_ROWS] = sums_ready[b]

        def project_out(b):
            gT = gatedT[b % 2]
            pe.wait(heads_gated[b], emptied[BANK_OUT[0]], emptied[BANK_OUT[1]])
            for c in range(CHUNKS):
                for j in range(TPS):
                    for r in range(P // DV):
                        rows = slice(r * DV, (r + 1) * DV)
                        col = (c * TPS + j) * D
                        m = pe.engine.matmul(banks[BANK_OUT[r]][:, col:col + D], gT[rows, c, j * P:(j + 1) * P],
                                             w_o_sb[rows, c, :], start=True, stop=True, tile_position=(r * DV, 0))
            projected_out[b] = pe.mark(m)

        def add_attention(b, rs_ready):
            dve.wait(rs_ready, projected_out[b])
            marks = [None] * TPS
            for h in range(HEADS):
                c, r = divmod(h, P // DV)
                for j in range(TPS):
                    t, col = TPS * b + j, (c * TPS + j) * D
                    dve.wait(marks[j])
                    marks[j] = dve.mark(dve.engine.scalar_tensor_tensor(
                        x_sb[:, t, :], banks[BANK_OUT[r]][:, col:col + D],
                        rs_out[:, COL_HEAD + j * HEADS + h:COL_HEAD + j * HEADS + h + 1], x_sb[:, t, :], ALU.mult, ALU.add))
            attended[b] = emptied[BANK_OUT[0]] = emptied[BANK_OUT[1]] = marks[-1]
            return layernorm_stats(range(TPS * b, TPS * (b + 1)), marks)

        ADD, NORM, PROJECT, SCORE, MIX, ATTEND, NORM2, GATES = range(8)

        def now(i, lag):
            return i - lag if 0 <= i - lag < SEQS else None

        rows2_stored = []
        pool.wait(slots_ready, *results_stored)
        for j in range(TPS):
            fetch(0, j)
        pe.wait(proj_ready, wo_ready)
        dve.wait(rope_in, scores_ready)
        values_ready = []
        rs_free = [rs_free]
        for i in range(SEQS + GATES):
            add, norm, proj, sc, mx, att, norm_2, gate = (now(i, lag) for lag in range(GATES + 1))
            if i + 1 < SEQS:
                for j in range(TPS):
                    fetch(0, TPS * (i + 1) + j)
            for m in values_ready:
                dve.wait(m)
            roots = rsqrt_steps(RS_N, None, rs_free) if values_ready else iter(())
            firsts, first_stats = add_first(add) if add is not None else ([], None)
            rs_ready, values_ready = None, []
            for between in (mask(mx) if mx is not None else []) + firsts:
                rs_ready = next(roots, None) or rs_ready
                between()
            for m in roots:
                rs_ready = m
            if proj is not None:
                xT_ready[proj] = transpose_rows(proj, proj % 2, split1[proj], BANK_ROWS)
            if gate is not None:
                x2T_ready = transpose_rows(gate, 2 + gate % 2, split2[gate], BANK_V)
            if mx is not None:
                mix(mx)
            if proj is not None:
                project_qk(proj)
            if norm is not None:
                norm1[norm] = normalise_on_act(norm, norm % 2, COL_X1, rs_ready, norm1.get(norm - 1))
            if norm_2 is not None:
                norm2[norm_2] = normalise_on_act(norm_2, 2 + norm_2 % 2, COL_X2, rs_ready, norm2.get(norm_2 - 1))
            if norm is not None:
                split1[norm] = rows_lo(norm % 2, rows_hi(norm % 2, norm1[norm]), pool)
            if norm_2 is not None:
                split2[norm_2] = rows_lo(2 + norm_2 % 2, rows_hi(2 + norm_2 % 2, norm2[norm_2]), pool)
                rows2_stored.append(store_rows(1, norm_2, 2 + norm_2 % 2, split2[norm_2]))
            if add is not None:
                values_ready.append(layernorm_value(COL_X1, TPS * add, TPS, first_stats(), rs_ready))
            if proj is not None:
                rotate(proj)
            if mx is not None:
                square_heads(mx)
                gate_heads(mx)
            if proj is not None:
                project_vg(proj)
            if mx is not None:
                sum_heads(mx, rs_ready)
                values_ready.append(sums_ready[mx])
            if gate is not None:
                logits_ready = gate_logits(gate, x2T_ready, gate_ready, BANK_ROWS, None)
            if sc is not None:
                score(sc)
            if att is not None:
                m = add_attention(att, rs_ready)
                values_ready.append(layernorm_value(COL_X2, TPS * att, TPS, m, rs_ready))
            if mx is not None:
                project_out(mx)
            rs_free = [m for m in (norm1.get(norm), norm2.get(norm_2), attended.get(att)) if m is not None] or [rs_ready]

        slots_ready, scores_ready, tokens_ready, offsets_ready = route(1, logits_ready)
        results_stored = experts(1, rows2_stored, tokens_ready, offsets_ready, None)
        out_tiles = out.rearrange("(t p) d -> p t d", p=P)
        out_store = Counter(None, sem("out_stored"), 16)
        pool.wait(slots_ready, *results_stored)
        dve.wait(scores_ready)
        for seq in range(SEQS):
            for j in range(TPS):
                fetch(1, TPS * seq + j)
            for j in range(TPS):
                m = add_back(1, TPS * seq + j)
            sp.wait_ge(*m)
            stored = out_store.mark(sp.dma_start(out_tiles[:, TPS * seq:TPS * (seq + 1), :], x_sb[:, TPS * seq:TPS * (seq + 1), :]))
        sp.wait_ge(*stored)


def kernel(**inputs):
    import concourse.bacc as bacc
    from concourse.bass_utils import run_bass_kernel_spmd

    a = {k: np.asarray(v) for k, v in inputs.items()}
    swap = np.arange(P).reshape(HEADS, 2, DK // 2)[:, ::-1].reshape(-1)
    wq, wk = a["L0_attn_Wq"], a["L0_attn_Wk"]
    arrays = {
        "x": a["L0_attn_x"].reshape(TOKENS, D),
        "w_proj": np.concatenate([wq, wq[swap], wk, wk[swap], a["L0_attn_Wv"], a["L0_attn_Wg"]]).T,
        "w_o": a["L0_attn_Wo"].T,
        "gnorm": np.tile(a["L0_attn_gnorm_w"], 2).reshape(P, 1),
        "w_redT": a["L0_ffn_w_red"].T,
        "wg": a["L0_ffn_wg"],
        "w1": a["L0_ffn_w1"],
        "b1T": a["L0_ffn_b1"].reshape(E * NF, P).T,
        "w2": a["L0_ffn_w2"],
        "b2": a["L0_ffn_b2"],
        "rope": rope_tables(),
        "consts": small_constants(),
        "halves": half_constants(),
        "masks": causal_mask(),
    }
    arrays = {k: np.ascontiguousarray(v) for k, v in arrays.items()}
    nc = bacc.Bacc("TRN2", target_bir_lowering=False, num_devices=1)
    args = [nc.dram_tensor(f"in_{k}", v.shape, mybir.dt.from_np(v.dtype), kind="ExternalInput").ap()
            for k, v in arrays.items()]
    out = nc.dram_tensor("out_x", (TOKENS, D), F32, kind="ExternalOutput").ap()
    macaron(nc, *args, out)
    r = run_bass_kernel_spmd(nc, [{f"in_{k}": v for k, v in arrays.items()}], core_ids=[0])
    return r.results[0]["out_x"].reshape(SEQS, T, D)
```

```python
from contextlib import ExitStack

import numpy as np

import concourse.bass as bass
from concourse import mybir

F32 = mybir.dt.float32
F16 = mybir.dt.float16
I32 = mybir.dt.int32
U32 = mybir.dt.uint32
ALU = mybir.AluOpType
ACT = mybir.ActivationFunctionType
AX = mybir.AxisListType

P = 128
SEQS, T, D = 8, 256, 128
TOKENS = SEQS * T
NT = TOKENS // P
TPS = T // P
E, F, GATE = 8, 512, 16
NF = F // P
NS = (TOKENS + E * (P - 1)) // P
HEADS, DK, DV = 4, 32, 64
VD = HEADS * DV
EPS = 1e-5
HEAD_COPIES = 64
ROW_SCALE = 16.0
WEIGHT_SCALE = 64.0
UNSCALE = 1.0 / (ROW_SCALE * WEIGHT_SCALE)
RSQRT_MAGIC = float(0x5F3759DF)
NEWTON_STEPS = 3

C_THRESH = 0
C_IOTA_E = C_THRESH + NT
C_IOTA_S = C_IOTA_E + E
C_BEFORE = C_IOTA_S + NS
C_TOKEN = C_BEFORE + E * E
C_BACK = C_TOKEN + NT
C_COLS = C_BACK + NS


def rope_tables():
    inv_freq = (1.0 / np.float32(10000.0) ** (np.arange(0, DK, 2, dtype=np.float32) / np.float32(DK))).astype(np.float32)
    angle = (np.arange(T, dtype=np.float32)[:, None] * inv_freq[None, :]).astype(np.float64)
    cos = np.tile(np.cos(angle).T, (2 * HEADS, 1))
    sin = np.tile(np.concatenate([-np.sin(angle).T, np.sin(angle).T]), (HEADS, 1))
    gamma = 1.0 - 2.0 ** (-5.0 - np.arange(HEADS))
    grow = np.repeat(gamma[:, None] ** np.arange(T)[None, :], DK, axis=0)
    q_factor = grow * DK ** -0.5 * UNSCALE
    k_factor = UNSCALE / grow
    table = np.stack([cos * q_factor, cos * k_factor, sin * q_factor, sin * k_factor], axis=1)
    return np.ascontiguousarray(table.reshape(P, 4 * T).astype(np.float32))


def small_constants():
    table = np.zeros((P, C_COLS), np.float32)
    table[:, C_THRESH:C_IOTA_E] = P * np.arange(NT)
    table[:, C_IOTA_E:C_IOTA_S] = np.arange(E) / E
    table[:, C_IOTA_S:C_BEFORE] = np.arange(NS)
    e = np.arange(E)
    table[:, C_BEFORE:C_TOKEN] = (e[None, :] < e[:, None]).astype(np.float32).reshape(-1)
    table[:, C_TOKEN:C_BACK] = P * np.arange(NT)[None, :] + np.arange(P)[:, None] + 1
    table[:, C_BACK:] = NS * P - 1 - (P * np.arange(NS)[None, :] + np.arange(P)[:, None])
    return table


def half_constants():
    i = np.arange(P)
    tile, expert = i // E, i % E
    parts = [
        i[:, None] == i[None, :],
        i[:, None] < i[None, :],
        (expert[:, None] == expert[None, :]) & (tile[:, None] < tile[None, :]),
        np.tile(i, (P, 1)),
        np.ones((P, P)),
        expert[:, None] == np.arange(E)[None, :],
    ]
    return np.concatenate([np.asarray(p, np.float16) for p in parts], axis=1)


def causal_mask():
    i = np.arange(P)
    causal = (i[:, None] <= i[None, :]).astype(np.float32)
    same_head = (i[:, None] // DV == i[None, ::DV // HEAD_COPIES] // DV).astype(np.float32)
    return np.concatenate([np.eye(P, dtype=np.float32), causal, np.ones((P, P), np.float32), causal, same_head], axis=1)

class Counter:

    def __init__(self, engine, sem, step=1):
        self.engine, self.sem, self.step, self.count = engine, sem, step, 0

    def mark(self, instruction):
        instruction.then_inc(self.sem, self.step)
        self.count += self.step
        return (self.sem, self.count)

    def wait(self, *marks):
        for m in marks:
            if m is not None:
                self.engine.wait_ge(*m)


def macaron(nc, x, w_proj, w_o, gnorm, w_redT, wg, w1, b1T, w2, b2, rope, consts, halves, masks, out):
    ctx = ExitStack()
    with ctx:
        ctx.enter_context(nc.allow_low_precision("float16 parts are exact splits"))

        def sb(name, shape, dt=F32):
            return ctx.enter_context(nc.sbuf_tensor(name, shape, dt))

        def ring(name, n, shape, dt=F32):
            return [sb(f"{name}{i}", shape, dt) for i in range(n)]

        def sem(name):
            return ctx.enter_context(nc.semaphore(name))

        def dma_counters(name, n):
            return [Counter(None, sem(f"{name}{i}"), 16) for i in range(n)]

        pe = Counter(nc.tensor, sem("tensor_done"))
        dve = Counter(nc.vector, sem("vector_done"))
        act = Counter(nc.scalar, sem("scalar_done"))
        pool = Counter(nc.gpsimd, sem("pool_done"))
        sp = nc.sync

        banks = [ctx.enter_context(nc.psum_tensor(f"bank{i}", [P, 512], F32)) for i in range(8)]
        emptied = [None] * 8

        c32 = sb("c32", [P, C_COLS])
        c16 = sb("c16", [P, 5 * P + E], F16)
        mask_sb = sb("mask_sb", [P, 4 * P + P // DV * HEAD_COPIES])
        rope_sb = sb("rope_sb", [P, 4 * T])
        ident16, before16, tile_before16, iota16, ones16 = (c16[:, k * P:(k + 1) * P] for k in range(5))
        expert16 = c16[:, 5 * P:5 * P + E]
        ident32, score_mask, head_rows = mask_sb[:, 0:P], mask_sb[:, P:4 * P], mask_sb[:, 4 * P:]

        x_sb = sb("x_sb", [P, NT, D])
        row_stats = sb("row_stats", [P, NT, 6])
        row_mean_var = sb("row_mean_var", [P, NT, 2])
        xnT = sb("xnT", [P, 2, TOKENS], F16)
        w_proj32 = sb("w_proj32", [P, 4 * P + 2 * VD])
        w_proj16 = sb("w_proj16", [P, 2, 4 * P + 2 * VD], F16)
        w_o_sb = sb("w_o_sb", [P, 2, D])
        gnorm_sb = sb("gnorm_sb", [P, 1])
        w_redT_sb = sb("w_redT_sb", [GATE, D])
        wg_sb = sb("wg_sb", [E, GATE])
        w_stage = sb("w_stage", [P, 2, E * F])
        w1_16 = sb("w1_16", [P, E * NF * 2 * P], F16)
        w2_16 = sb("w2_16", [P, E * NF * 2 * D], F16)
        b1_sb = sb("b1_sb", [P, E * NF])
        b2_sb = sb("b2_sb", [P, E * D])

        rows_dram = [nc.dram_tensor(f"rows{k}", [TOKENS, 2 * D], F16) for k in range(2)]
        y_by_slot = nc.dram_tensor("y_by_slot", [NS * P, D], F32)

        def load(name, dst, src):
            return Counter(None, sem(f"load_{name}"), 16).mark(sp.dma_start(dst, src))

        LOADS = 2
        x_tiles = x.rearrange("(t p) d -> p t d", p=P)
        x_in = []
        for g in range(LOADS):
            n = NT // LOADS
            x_in.append(load(f"x{g}", x_sb[:, g * n:(g + 1) * n, :], x_tiles[:, g * n:(g + 1) * n, :]))
            if g == 0:
                wg_in = load("wg", wg_sb[:, :], wg)
                w_redT_in = load("w_redT", w_redT_sb[:, :], w_redT)
                masks_in = load("masks", mask_sb[:, :], masks)
                halves_in = load("halves", c16[:, :], halves)
        W_PARTS = 4
        ep = E // W_PARTS
        w1_in, w2_in = [], []
        for g in range(W_PARTS):
            cols = slice(g * ep * F, (g + 1) * ep * F)
            w1_in.append(load(f"w1_{g}", w_stage[:, 0, cols].rearrange("p (e f) -> p e f", e=ep),
                              w1[g * ep:(g + 1) * ep].rearrange("e d f -> d e f")))
        consts_in = load("consts", c32[:, :], consts)
        b1_in = load("b1", b1_sb[:, :], b1T)
        for g in range(W_PARTS):
            cols = slice(g * ep * F, (g + 1) * ep * F)
            w2_in.append(load(f"w2_{g}", w_stage[:, 1, cols].rearrange("p (m d) -> p m d", d=D),
                              w2[g * ep:(g + 1) * ep].rearrange("e (j p) d -> p (e j) d", p=P)))
        b2_in = load("b2", b2_sb[:, :], b2.rearrange("(o e) d -> o (e d)", o=1).broadcast_to([P, E * D]))
        proj_in = load("w_proj", w_proj32[:, :], w_proj)
        wo_in = load("w_o", w_o_sb[:, :, :], w_o.rearrange("(k p) d -> p k d", p=P))
        gnorm_in = load("gnorm", gnorm_sb[:, :], gnorm)
        rope_in = load("rope", rope_sb[:, :], rope)

        rs_val, rs_tmp, rs_out = (sb(name, [P, NT + 1]) for name in ("rs_val", "rs_tmp", "rs_out"))
        rs_int = sb("rs_int", [P, NT + 1], I32)

        def rsqrt_steps(n, ready, out_read):
            v, t, y, i = rs_val[:, 0:n], rs_tmp[:, 0:n], rs_out[:, 0:n], rs_int[:, 0:n]
            dve.wait(ready)
            m = dve.mark(dve.engine.tensor_scalar(i, v.bitcast(I32), 1, None, ALU.logical_shift_right))
            yield m
            dve.wait(m, *out_read)
            m = dve.mark(dve.engine.tensor_scalar(y.bitcast(I32), i, -1.0, RSQRT_MAGIC, ALU.mult, ALU.add))
            yield m
            for _ in range(NEWTON_STEPS):
                dve.wait(m)
                m = dve.mark(dve.engine.tensor_tensor(t, y, v, ALU.mult))
                yield m
                dve.wait(m)
                m = dve.mark(dve.engine.scalar_tensor_tensor(t, t, -0.5, y, ALU.mult, ALU.mult))
                yield m
                dve.wait(m)
                m = dve.mark(dve.engine.scalar_tensor_tensor(y, t, 1.5, y, ALU.add, ALU.mult))
                yield m

        gate_sq = sb("gate_sq", [E, GATE])
        gate_ss = sb("gate_ss", [E, 1])
        gate_wn = sb("gate_wn", [E, GATE])
        gate_wnT = sb("gate_wnT", [GATE, E])
        gate_w32 = sb("gate_w32", [P, E])
        gate_w16 = sb("gate_w16", [P, 2, E], F16)

        COL_GATE = NT

        def gate_norms():
            ones = dve.mark(dve.engine.memset(rs_val[:, :], 1.0))
            dve.wait(wg_in)
            m = dve.mark(dve.engine.tensor_tensor(gate_sq[:, :], wg_sb[:, :], wg_sb[:, :], ALU.mult))
            dve.wait(m)
            m = dve.mark(dve.engine.tensor_reduce(gate_ss[:, :], gate_sq[:, :], AX.X, ALU.add))
            dve.wait(m, ones)
            return dve.mark(dve.engine.tensor_scalar(rs_val[0:E, COL_GATE:COL_GATE + 1], gate_ss[:, :], 1e-8, None, ALU.max))

        def gate_columns(rs_ready):
            dve.wait(rs_ready)
            m = dve.mark(dve.engine.tensor_scalar(gate_wn[:, :], wg_sb[:, :], rs_out[0:E, COL_GATE:COL_GATE + 1], None, ALU.mult))
            pe.wait(m, masks_in)
            m = pe.mark(pe.engine.transpose(banks[7][0:GATE, 0:E], gate_wn[:, :], ident32[0:E, 0:E]))
            act.wait(m)
            emptied[7] = act.mark(act.engine.activation(gate_wnT[:, :], banks[7][0:GATE, 0:E], ACT.Copy))
            return emptied[7]

        def gate_weights(columns):
            pe.wait(columns, w_redT_in)
            m = pe.mark(pe.engine.matmul(banks[6][:, 0:E], w_redT_sb[:, :], gate_wnT[:, :], start=True, stop=True))
            act.wait(m)
            emptied[6] = act.mark(act.engine.activation(gate_w32[:, :], banks[6][:, 0:E], ACT.Copy, scale=WEIGHT_SCALE))
            act.wait(emptied[6])
            m = act.mark(act.engine.activation(gate_w16[:, 0, :], gate_w32[:, :], ACT.Copy))
            pool.wait(m)
            return pool.mark(pool.engine.tensor_tensor(gate_w16[:, 1, :], gate_w32[:, :], gate_w16[:, 0, :], ALU.subtract))

        def scaled_weights_hi(hi, src, loaded):
            act.wait(loaded)
            scaled = act.mark(act.engine.activation(src, src, ACT.Copy, scale=WEIGHT_SCALE))
            act.wait(scaled)
            return act.mark(act.engine.activation(hi, src, ACT.Copy))

        def scaled_weights_lo(lo, src, hi, hi_ready):
            pool.wait(hi_ready)
            return pool.mark(pool.engine.tensor_tensor(lo, src, hi, ALU.subtract))

        def part_of(w16, which, g):
            src = w_stage[:, which, g * ep * F:(g + 1) * ep * F].rearrange("p (m c) -> p m c", c=P)
            dst = w16[:, g * ep * 2 * F:(g + 1) * ep * 2 * F].rearrange("p (m h c) -> p m h c", h=2, c=P)
            return src, dst[:, :, 0, :], dst[:, :, 1, :]

        def split_w1(g):
            src, hi, lo = part_of(w1_16, 0, g)
            return scaled_weights_lo(lo, src, hi, scaled_weights_hi(hi, src, w1_in[g]))

        def w2_hi(g):
            src, hi, lo = part_of(w2_16, 1, g)
            act.wait(w2_in[g])
            return act.mark(act.engine.activation(hi, src, ACT.Copy, scale=WEIGHT_SCALE))

        def w2_lo(g, hi_ready):
            src, hi, lo = part_of(w2_16, 1, g)
            dve.wait(w2_in[g], hi_ready)
            return dve.mark(dve.engine.scalar_tensor_tensor(lo, src, WEIGHT_SCALE, hi, ALU.mult, ALU.subtract))

        def layernorm_stats(tiles, ready):
            marks = []
            for t, m in zip(tiles, ready):
                dve.wait(m)
                marks.append(dve.mark(dve.engine.bn_stats(row_stats[:, t, :], x_sb[:, t, :])))
            for t, m in zip(tiles, marks):
                dve.wait(m)
                m = dve.mark(dve.engine.bn_aggr(row_mean_var[:, t, :], row_stats[:, t, :]))
            return m

        def layernorm_value(col, t0, n, stats_ready, val_read):
            k = ROW_SCALE ** -2
            dve.wait(stats_ready, val_read)
            return dve.mark(dve.engine.tensor_scalar(rs_val[:, col:col + n], row_mean_var[:, t0:t0 + n, 1],
                                                     k, EPS * k, ALU.mult, ALU.add))

        ROW_BUFS = SEQS
        xn32 = ring("xn32_", ROW_BUFS, [P, TPS, D])
        xn16 = ring("xn16_", ROW_BUFS, [P, TPS, 2, D], F16)
        rows_store = dma_counters("rows_stored", ROW_BUFS)
        xn32_read = [None] * ROW_BUFS
        xn16_transposed = [None] * ROW_BUFS
        xn16_stored = [None] * ROW_BUFS

        def normalise(seq, buf, col, rs_ready):
            n32 = xn32[buf]
            dve.wait(rs_ready, xn32_read[buf])
            for j in range(TPS):
                t = TPS * seq + j
                m = dve.mark(dve.engine.tensor_scalar(n32[:, j, :], x_sb[:, t, :], row_mean_var[:, t, 0:1],
                                                      rs_out[:, col + j:col + j + 1], ALU.subtract, ALU.mult))
            return m

        def rows_hi(buf, normalised):
            act.wait(normalised, xn16_transposed[buf], xn16_stored[buf])
            return act.mark(act.engine.activation(xn16[buf][:, :, 0, :], xn32[buf][:, :, :], ACT.Copy))

        def rows_lo(buf, hi, lo_engine):
            n32, n16 = xn32[buf], xn16[buf]
            lo_engine.wait(hi)
            lo = lo_engine.mark(lo_engine.engine.tensor_tensor(n16[:, :, 1, :], n32[:, :, :], n16[:, :, 0, :], ALU.subtract))
            xn32_read[buf] = lo
            return lo

        def store_rows(k, seq, buf, split):
            sp.wait_ge(*split)
            rows = rows_dram[k].ap().rearrange("(t p) c -> p t c", p=P)[:, TPS * seq:TPS * (seq + 1), :]
            xn16_stored[buf] = rows_store[buf].mark(
                sp.dma_start(rows, xn16[buf][:, :, :, :].rearrange("p t h d -> p t (h d)")))
            return xn16_stored[buf]

        xnT_read = [None] * SEQS

        def transpose_rows(seq, buf, split, b):
            n16 = xn16[buf]
            b16 = banks[b][:, :].bitcast(F16)
            pe.wait(split, halves_in, emptied[b])
            for h in range(2):
                for j in range(TPS):
                    c = (h * TPS + j) * P
                    m = pe.engine.transpose(b16[:, c:c + P], n16[:, j, h, :], ident16)
            m = pe.mark(m)
            xn16_transposed[buf] = m
            act.wait(m, xnT_read[seq])
            m = act.mark(act.engine.activation(xnT[:, :, seq * T:(seq + 1) * T],
                                               b16[:, 0:2 * T].rearrange("p (h t) -> p h t", h=2), ACT.Copy))
            emptied[b] = m
            return m

        logits = sb("logits", [P, NT, E])

        def gate_matmuls(seq, xT_ready, w_ready, b):

            def product(j, rows, weights, first, last):
                if j == 0 and first:
                    pe.wait(xT_ready, w_ready, emptied[b])
                t = TPS * seq + j
                m = pe.engine.matmul(banks[b][:, j * E:(j + 1) * E], xnT[:, rows, t * P:(t + 1) * P], gate_w16[:, weights, :],
                                     start=first, stop=last)
                if j == TPS - 1 and last:
                    xnT_read[seq] = pe.mark(m)

            return [lambda j=j, a=a: product(j, *a) for j in range(TPS)
                    for a in ((0, 0, True, False), (0, 1, False, False), (1, 0, False, True))]

        def gate_logits(seq, b):
            act.wait(xnT_read[seq])
            m = act.mark(act.engine.activation(logits[:, TPS * seq:TPS * (seq + 1), :],
                                               banks[b][:, 0:TPS * E].rearrange("p (t e) -> p t e", e=E),
                                               ACT.Copy, scale=UNSCALE))
            emptied[b] = m
            return m

        shape_te = [P, NT, E]
        r_max = sb("r_max", [P, NT])
        r_shift = sb("r_shift", shape_te)
        r_exp = sb("r_exp", shape_te)
        r_sum = sb("r_sum", [P, NT])
        half_score = [sb(f"half_score{k}", [P, NT]) for k in range(2)]
        r_cand = sb("r_cand", shape_te)
        r_expert = sb("r_expert", [P, NT])
        member = sb("member", shape_te, F16)
        count16 = sb("count16", [P, P], F16)
        r_rank = sb("r_rank", shape_te)
        r_total = sb("r_total", [P, E])
        r_cmp = sb("r_cmp", [P, E, NT])
        r_tiles = sb("r_tiles", [P, E])
        r_tri = sb("r_tri", [P, E, E])
        r_start = sb("r_start", [P, E])
        r_posf = sb("r_posf", [P, NT])
        slot_of = sb("slot_of", [P, NT], U32)
        place_of = sb("place_of", [P, NS], U32)
        r_unused = sb("r_unused", [P, NS])
        score16 = sb("score16", [P, 2, NT], F16)
        tile_score = sb("tile_score", [P, NT, 2, NS], F16)
        score_of = sb("score_of", [P, NS])
        r_posi = sb("r_posi", [P, NT], I32)
        r_rowi = sb("r_rowi", [P, NT], I32)
        r_tilei = sb("r_tilei", [P, NT], I32)
        r_rowf = sb("r_rowf", [P, NT])
        r_tilef = sb("r_tilef", [P, NT])
        row_hot = sb("row_hot", [P, NT, P], F16)
        tile_hot = sb("tile_hot", [P, NT, NS])
        tile_token = sb("tile_token", [P, NT, NS], F16)
        token_of = [sb(f"token_of{k}", [P, NS], U32) for k in range(2)]
        s_cmp = sb("s_cmp", [1, NS, E - 1])
        s_expert = sb("s_expert", [1, NS])
        offsets = [sb(f"offsets{k}", [1, 3, NS], I32) for k in range(2)]
        OFF_W, OFF_B1, OFF_B2 = range(3)

        def step(instruction):
            m = dve.mark(instruction)
            dve.wait(m)
            return m

        def choose(t0, t1, logits_ready):
            v, ts = dve.engine, slice(t0, t1)
            shape = [P, t1 - t0, E]

            def over_experts(a):
                return a.unsqueeze(2).broadcast_to(shape)

            dve.wait(logits_ready, consts_in)
            step(v.tensor_reduce(r_max[:, ts], logits[:, ts, :], AX.X, ALU.max))
            shifted = step(v.tensor_tensor(r_shift[:, ts, :], logits[:, ts, :], over_experts(r_max[:, ts]), ALU.subtract))
            iota_e = c32[:, C_IOTA_E:C_IOTA_S].unsqueeze(1).broadcast_to(shape)
            step(v.scalar_tensor_tensor(r_cand[:, ts, :], r_shift[:, ts, :], 0.0, iota_e, ALU.is_lt, ALU.add))
            step(v.tensor_reduce(r_expert[:, ts], r_cand[:, ts, :], AX.X, ALU.min))
            chosen = step(v.tensor_tensor(member[:, ts, :], iota_e, over_experts(r_expert[:, ts]), ALU.is_equal))
            return shifted, chosen

        def route(k, shifted, chosen):
            v = dve.engine
            act.wait(shifted)
            exps = act.mark(act.engine.activation(r_exp[:, :, :], r_shift[:, :, :], ACT.Exp))
            members = member[:, :, :].rearrange("p t e -> p (t e)")
            counts, ranks, tokens = banks[0], banks[1], banks[2]
            pe.wait(chosen, emptied[0])
            m = pe.mark(pe.engine.matmul(counts[:, 0:P], members, ones16, start=True, stop=True))
            dve.wait(m)
            m = dve.mark(v.tensor_copy(count16[:, :], counts[:, 0:P]))
            emptied[0] = m
            pe.wait(m, emptied[1])
            pe.engine.matmul(ranks[:, P:P + E], count16[:, :], expert16, start=True, stop=True)
            pe.engine.matmul(ranks[:, 0:P], before16, members, start=True, stop=False)
            ranked = pe.mark(pe.engine.matmul(ranks[:, 0:P], count16[:, :], tile_before16, start=False, stop=True))
            dve.wait(ranked)
            own = step(v.tensor_tensor(r_rank[:, :, :], ranks[:, 0:P].rearrange("p (t e) -> p t e", e=E), member[:, :, :], ALU.mult))
            totals = dve.mark(v.tensor_copy(r_total[:, :], ranks[:, P:P + E]))
            emptied[1] = totals
            own_rank = dve.mark(v.tensor_reduce(r_posf[:, :], r_rank[:, :, :], AX.X, ALU.add))
            thresholds = c32[:, C_THRESH:C_IOTA_E].unsqueeze(1).broadcast_to([P, E, NT])
            dve.wait(totals)
            compared = dve.mark(v.tensor_tensor(r_cmp[:, :, :], r_total[:, :].unsqueeze(2).broadcast_to([P, E, NT]), thresholds, ALU.is_gt))
            dve.wait(own_rank)
            rank_int = dve.mark(v.tensor_copy(r_posi[:, :], r_posf[:, :]))
            dve.wait(compared)
            tiles_known = dve.mark(v.tensor_reduce(r_tiles[:, :], r_cmp[:, :, :], AX.X, ALU.add))
            dve.wait(rank_int)
            row_int = dve.mark(v.tensor_scalar(r_rowi[:, :], r_posi[:, :], P - 1, None, ALU.bitwise_and))
            tile_int = dve.mark(v.tensor_scalar(r_tilei[:, :], r_posi[:, :], 7, None, ALU.logical_shift_right))
            before = c32[:, C_BEFORE:C_TOKEN].rearrange("p (a b) -> p a b", a=E)
            dve.wait(tiles_known)
            earlier = dve.mark(v.tensor_tensor(r_tri[:, :, :], r_tiles[:, :].unsqueeze(1).broadcast_to([P, E, E]), before, ALU.mult))
            dve.wait(row_int)
            row_known = dve.mark(v.tensor_copy(r_rowf[:, :], r_rowi[:, :]))
            dve.wait(tile_int)
            rank_tile = dve.mark(v.tensor_copy(r_tilef[:, :], r_tilei[:, :]))

            row_ready = {}

            def row_mask(t):
                row_ready[t] = dve.mark(v.tensor_scalar(row_hot[:, t, :], iota16, r_rowf[:, t:t + 1], None, ALU.is_equal))

            dve.wait(earlier)
            started = dve.mark(v.tensor_reduce(r_start[:, :], r_tri[:, :, :], AX.X, ALU.add))
            dve.wait(row_known)
            row_mask(0)
            dve.wait(started)
            m = dve.mark(v.tensor_tensor(r_rank[:, :, :], r_start[:, :].unsqueeze(1).broadcast_to(shape_te), member[:, :, :], ALU.mult))
            row_mask(1)
            dve.wait(m)
            m = dve.mark(v.tensor_reduce(r_posf[:, :], r_rank[:, :, :], AX.X, ALU.add))
            row_mask(2)
            dve.wait(m, rank_tile)
            located = dve.mark(v.tensor_tensor(r_tilef[:, :], r_posf[:, :], r_tilef[:, :], ALU.add))
            row_mask(3)
            shape_ts = [P, NT, NS]
            iota_ts = c32[:, C_IOTA_S:C_BEFORE].unsqueeze(1).broadcast_to(shape_ts)
            dve.wait(located)
            hot = dve.mark(v.tensor_tensor(tile_hot[:, :, :], iota_ts, r_tilef[:, :].unsqueeze(2).broadcast_to(shape_ts), ALU.is_equal))
            row_mask(4)
            dve.wait(hot)
            tile_ready = dve.mark(v.tensor_tensor(tile_token[:, :, :], tile_hot[:, :, :],
                                                  c32[:, C_TOKEN:C_BACK].unsqueeze(2).broadcast_to(shape_ts), ALU.mult))
            pe.wait(tile_ready, emptied[2])
            for t in range(NT):
                if t > 4:
                    row_mask(t)
                pe.wait(row_ready[t])
                m = pe.engine.matmul(tokens[:, 0:NS], row_hot[:, t, :], tile_token[:, t, :], start=(t == 0), stop=(t == NT - 1))
            inverted = pe.mark(m)
            iota_s = c32[0:1, C_IOTA_S:C_BEFORE].unsqueeze(2).broadcast_to([1, NS, E - 1])
            starts = r_start[0:1, 1:E].unsqueeze(1).broadcast_to([1, NS, E - 1])
            step(v.tensor_tensor(s_cmp[:, :, :], starts, iota_s, ALU.is_le))
            dve.wait(inverted)
            tokens_ready = dve.mark(v.tensor_scalar(token_of[k][:, :], tokens[:, 0:NS], 1.0, 0.0, ALU.subtract, ALU.max))
            step(v.tensor_reduce(s_expert[:, :], s_cmp[:, :, :], AX.X, ALU.add))
            for row, unit in ((OFF_W, 2 * F), (OFF_B1, NF), (OFF_B2, D)):
                offsets_ready = dve.mark(v.tensor_scalar(offsets[k][:, row, :], s_expert[:, :], float(unit), None, ALU.mult))
            if k == 0:
                step(v.tensor_scalar(r_tilef[:, :], r_tilef[:, :], float(P), None, ALU.mult))
                places_ready = dve.mark(v.tensor_tensor(slot_of[:, :], r_tilef[:, :], r_rowf[:, :], ALU.add))
            else:
                step(v.scalar_tensor_tensor(r_unused[:, :], tokens[:, 0:NS], 0.0, c32[:, C_BACK:C_COLS], ALU.is_equal, ALU.mult))
                places_ready = dve.mark(v.scalar_tensor_tensor(place_of[:, :], tokens[:, 0:NS], float(NS * P - 1), r_unused[:, :],
                                                               ALU.add, ALU.subtract))
            emptied[2] = places_ready
            dve.wait(exps)
            step(v.tensor_reduce(r_sum[:, :], r_exp[:, :, :], AX.X, ALU.add))
            step(v.reciprocal(half_score[k][:, :], r_sum[:, :]))
            scores_ready = dve.mark(v.tensor_scalar(half_score[k][:, :], half_score[k][:, :], 0.5, None, ALU.mult))
            return places_ready, scores_ready, tokens_ready, offsets_ready

        BANK_SCORE_OF = 5

        def scores_of_slots(scores_ready):
            v, bank = dve.engine, banks[BANK_SCORE_OF]
            shape_ts = [P, NT, NS]
            dve.wait(scores_ready)
            step(v.tensor_copy(score16[:, 0, :], half_score[1][:, :]))
            step(v.tensor_tensor(score16[:, 1, :], half_score[1][:, :], score16[:, 0, :], ALU.subtract))
            for part in range(2):
                m = dve.mark(v.tensor_tensor(tile_score[:, :, part, :], tile_hot[:, :, :],
                                             score16[:, part, :].unsqueeze(2).broadcast_to(shape_ts), ALU.mult))
            pe.wait(m, emptied[BANK_SCORE_OF])
            for t in range(NT):
                m = pe.engine.matmul(bank[:, 0:2 * NS], row_hot[:, t, :], tile_score[:, t, :, :].rearrange("p h s -> p (h s)"),
                                     start=(t == 0), stop=(t == NT - 1))
            m = pe.mark(m)
            dve.wait(m)
            hi = dve.mark(v.tensor_copy(score_of[:, :], bank[:, 0:NS]))
            dve.wait(hi)
            emptied[BANK_SCORE_OF] = dve.mark(v.tensor_tensor(score_of[:, :], bank[:, NS:2 * NS], score_of[:, :], ALU.add))
            return emptied[BANK_SCORE_OF]

        GATHERS, SLOTS_T, HIDDEN, RESULTS = 8, 3, 3, 6
        slot_rows = ring("slot_rows", GATHERS, [P, 2, D], F16)
        gather_done = dma_counters("gathered", GATHERS)
        slotT = ring("slotT", SLOTS_T, [P, 2, P], F16)
        hidden32 = ring("hidden32_", HIDDEN, [P, NF, P])
        hidden16 = ring("hidden16_", HIDDEN, [P, 2, NF, P], F16)
        y_sb = ring("y_sb", RESULTS, [P, D])
        y_store, y_scatter = dma_counters("y_stored", RESULTS), dma_counters("y_scattered", RESULTS)
        BANK_T, BANK_UP, BANK_DOWN = (0, 1, 7), (2, 3, 4), (5, 6)
        table_out = sb("table_out", [P, 1])
        gathered, transposed, t_copied, up_done, activated, hidden_split, down_done, y_stored = ({} for _ in range(8))

        def load_offsets(eng, k, row, limit, ready):
            regs = [eng.engine.alloc_register(f"off{k}_{row}_{i}") for i in range(NS)]
            eng.wait(ready)
            eng.engine.reg_load(regs, offsets[k][0:1, row, :])
            return [eng.engine.snap(r, min_val=0, max_val=limit) for r in regs]

        def experts(k, rows_stored, tokens_ready, offsets_ready, w1_ready, w2_ready, places_ready=None, out_ready=(), scores_of_slots=None):
            scores_by_slot = []
            s0, s1 = k * NS, (k + 1) * NS
            w_off = load_offsets(pe, k, OFF_W, (E - 1) * 2 * F, offsets_ready)
            b1_off = load_offsets(act, k, OFF_B1, (E - 1) * NF, offsets_ready)
            b2_off = load_offsets(dve, k, OFF_B2, (E - 1) * D, offsets_ready)
            pool.wait(tokens_ready, *rows_stored)
            pe.wait(w1_ready, *(emptied[b] for b in BANK_T + BANK_UP + BANK_DOWN))
            act.wait(b1_in)
            dve.wait(b2_in)

            def gather(s):
                pool.wait(transposed.get(s - GATHERS))
                gathered[s] = gather_done[s % GATHERS].mark(pool.engine.indirect_dma_start(
                    slot_rows[s % GATHERS][:, :, :].rearrange("p h d -> p (h d)"), None, rows_dram[k].ap(),
                    bass.IndirectOffsetOnAxis(token_of[k][:, s - s0:s - s0 + 1], 0)))

            def transpose(s):
                rows, t16 = slot_rows[s % GATHERS], slotT[s % SLOTS_T]
                b = BANK_T[s % len(BANK_T)]
                b16 = banks[b][:, :].bitcast(F16)
                pe.wait(gathered[s])
                pe.engine.transpose(b16[:, 0:P], rows[:, 0, :], ident16)
                transposed[s] = pe.mark(pe.engine.transpose(b16[:, P:2 * P], rows[:, 1, :], ident16))
                act.wait(transposed[s], up_done.get(s - SLOTS_T))
                t_copied[s] = act.mark(act.engine.activation(t16[:, :, :], b16[:, 0:2 * P].rearrange("p (h t) -> p h t", h=2), ACT.Copy))
                emptied[b] = t_copied[s]

            def up(s):
                hi, lo = slotT[s % SLOTS_T][:, 0, :], slotT[s % SLOTS_T][:, 1, :]
                b = BANK_UP[s % len(BANK_UP)]
                pe.wait(t_copied[s])
                for f in range(NF):
                    o = banks[b][:, f * P:(f + 1) * P]
                    w_hi, w_lo = (w1_16[:, bass.ds(w_off[s - s0] + (2 * f + part) * P, P)] for part in range(2))
                    pe.engine.matmul(o, w_hi, hi, start=True, stop=False)
                    pe.engine.matmul(o, w_hi, lo, start=False, stop=False)
                    m = pe.engine.matmul(o, w_lo, hi, start=False, stop=True)
                up_done[s] = pe.mark(m)

            def activate(s):
                h = hidden32[s % HIDDEN]
                b = BANK_UP[s % len(BANK_UP)]
                act.wait(up_done[s], hidden_split.get(s - HIDDEN))
                bias = b1_sb[:, bass.ds(b1_off[s - s0], NF)]
                for f in range(NF):
                    m = act.mark(act.engine.activation(h[:, f, :], banks[b][:, f * P:(f + 1) * P], ACT.Gelu,
                                                       bias=bias[:, f:f + 1], scale=UNSCALE))
                activated[s] = emptied[b] = m

            hi_ready, half_ready = {}, {}

            def split_hi(s):
                h, parts = hidden32[s % HIDDEN], hidden16[s % HIDDEN]
                dve.wait(activated[s], down_done.get(s - HIDDEN))
                hi_ready[s] = dve.mark(dve.engine.tensor_copy(parts[:, 0, :, :], h[:, :, :]))

            def split_lo(s):
                h, parts = hidden32[s % HIDDEN], hidden16[s % HIDDEN]
                dve.wait(hi_ready[s])
                hidden_split[s] = dve.mark(dve.engine.tensor_tensor(parts[:, 1, :, :], h[:, :, :], parts[:, 0, :, :], ALU.subtract))

            def down(s):
                parts = hidden16[s % HIDDEN]
                b = BANK_DOWN[s % len(BANK_DOWN)]
                pe.wait(hidden_split[s])
                for f in range(NF):
                    w = w2_16[:, bass.ds(w_off[s - s0] + 2 * f * D, 2 * D)]
                    if f == 0:
                        pe.engine.matmul(banks[b][:, 0:2 * D], parts[:, 0, f, :], w, start=True, stop=False)
                    pe.engine.matmul(banks[b][:, 0:D], parts[:, 1, f, :], w[:, 0:D], start=False, stop=False)
                    if f > 0:
                        m = pe.engine.matmul(banks[b][:, 0:2 * D], parts[:, 0, f, :], w, start=False, stop=(f == NF - 1))
                down_done[s] = pe.mark(m)

            def finish_half(s):
                y = y_sb[s % RESULTS]
                b = BANK_DOWN[s % len(BANK_DOWN)]
                dve.wait(down_done[s], y_stored.get(s - RESULTS))
                half_ready[s] = dve.mark(dve.engine.scalar_tensor_tensor(y[:, :], banks[b][:, 0:D], 1.0 / WEIGHT_SCALE,
                                                                         b2_sb[:, bass.ds(b2_off[s - s0], D)], ALU.mult, ALU.add))

            def finish(s):
                y = y_sb[s % RESULTS]
                b = BANK_DOWN[s % len(BANK_DOWN)]
                dve.wait(half_ready[s])
                m = dve.mark(dve.engine.scalar_tensor_tensor(y[:, :], banks[b][:, D:2 * D], 1.0 / WEIGHT_SCALE,
                                                             y[:, :], ALU.mult, ALU.add))
                emptied[b] = m
                if k == 0:
                    sp.wait_ge(*m)
                    store = sp.dma_start(y_by_slot.ap()[(s - s0) * P:(s - s0 + 1) * P, :], y[:, :])
                else:
                    act.wait(m, scores_by_slot[0])
                    m = act.mark(act.engine.activation(y[:, :], y[:, :], ACT.Copy, scale=score_of[:, s - s0:s - s0 + 1]))
                    pool.wait(m)
                    if s == s0:
                        pool.wait(places_ready, *out_ready)
                    store = pool.engine.indirect_dma_start(out, bass.IndirectOffsetOnAxis(place_of[:, s - s0:s - s0 + 1], 0),
                                                           y[:, :], None, compute_op=ALU.add)
                y_stored[s] = (y_store, y_scatter)[k][s % RESULTS].mark(store)

            T_AHEAD = SLOTS_T - 1
            for s in range(s0, s0 + GATHERS - 1):
                gather(s)
            for s in range(s0, s0 + T_AHEAD):
                transpose(s)
            act.engine.activation(table_out[:, :], b1_sb[:, 0:1], ACT.Gelu)
            for s in range(s0, s1 + 3):
                if s + GATHERS - 1 < s1:
                    gather(s + GATHERS - 1)
                if s < s1:
                    up(s)
                    activate(s)
                if s + T_AHEAD < s1:
                    transpose(s + T_AHEAD)
                if s == s0:
                    pe.wait(*w2_ready)
                    if k == 1:
                        scores_by_slot.append(scores_of_slots())
                        pe.wait(scores_by_slot[0])
                if s0 <= s - 2 < s1:
                    down(s - 2)
                if s0 <= s - 3:
                    finish_half(s - 3)
                if s0 <= s - 1 < s1:
                    split_hi(s - 1)
                if s0 <= s - 3:
                    finish(s - 3)
                if s0 <= s - 1 < s1:
                    split_lo(s - 1)
            return [y_stored[s] for s in range(s1 - RESULTS, s1)]

        BACK = 6
        back = ring("back", BACK, [P, D])
        back_landed = dma_counters("back_landed", BACK)
        fetched, added_back = {}, {}

        def fetch(k, t):
            n = k * NT + t
            pool.wait(added_back.get(n - BACK))
            fetched[n] = back_landed[n % BACK].mark(pool.engine.indirect_dma_start(
                back[n % BACK][:, :], None, y_by_slot.ap(), bass.IndirectOffsetOnAxis(slot_of[:, t:t + 1], 0)))

        def add_back(k, t, x_ready=None):
            n = k * NT + t
            dve.wait(fetched[n], x_ready)
            added_back[n] = dve.mark(dve.engine.scalar_tensor_tensor(x_sb[:, t, :], back[n % BACK][:, :], half_score[k][:, t:t + 1],
                                                                     x_sb[:, t, :], ALU.mult, ALU.add))
            return added_back[n]

        rows_stored = []
        group = NT // LOADS
        seqs = group // TPS
        zeros = sb("zeros", [P, D])
        zeroed = pool.mark(pool.engine.memset(zeros[:, :], 0.0))
        gate_value = gate_norms()
        rows_stored = []
        w1_ready = split_w1(0)
        group = NT // LOADS
        for g in range(LOADS):
            m = layernorm_stats(range(g * group, (g + 1) * group), [x_in[g]] + [None] * (group - 1))
        m = layernorm_value(0, 0, NT, m, None)
        dve.wait(gate_value)
        *_, rs_ready = rsqrt_steps(NT + 1, m, [])
        hi, split, xT = {}, {}, {}
        for i in range(SEQS + 2):
            if i < SEQS:
                normalised = normalise(i, i, TPS * i, rs_ready)
                hi[i] = rows_hi(i, normalised)
            if i == 0:
                columns = gate_columns(rs_ready)
            if i == 1:
                gate_ready = gate_weights(columns)
            if 0 <= i - 1 < SEQS:
                split[i - 1] = rows_lo(i - 1, hi[i - 1], dve)
                rows_stored.append(store_rows(0, i - 1, i - 1, split[i - 1]))
                xT[i - 1] = transpose_rows(i - 1, i - 1, split[i - 1], (i - 1) % 4)
            if 0 <= i - 2 < SEQS:
                for product in gate_matmuls(i - 2, xT[i - 2], gate_ready, 4 + (i - 2) % 4):
                    product()
                logits_ready = gate_logits(i - 2, 4 + (i - 2) % 4)
            if i - 2 == SEQS // 2 - 1:
                half_logits = logits_ready
        rs_free = split[SEQS - 1]
        for part in range(1, W_PARTS):
            w1_ready = split_w1(part)
        hi_ready = [w2_hi(part) for part in range(W_PARTS - 1)]
        choose(0, NT // 2, half_logits)
        slots_ready, scores_ready, tokens_ready, offsets_ready = route(0, *choose(NT // 2, NT, logits_ready))
        hi_ready.append(w2_hi(W_PARTS - 1))
        w2_ready = [w2_lo(part, hi_ready[part]) for part in range(W_PARTS)]
        proj_hi = scaled_weights_hi(w_proj16[:, 0, :], w_proj32[:, :], proj_in)
        sp.wait_ge(*zeroed)
        out_ready = [Counter(None, sem("empty_rows_zeroed"), 16).mark(
            sp.dma_start(out[0:NS * P, :].rearrange("(s p) d -> p s d", p=P), zeros[:, :].unsqueeze(1).broadcast_to([P, NS, D])))]
        results_stored = experts(0, rows_stored, tokens_ready, offsets_ready, w1_ready, w2_ready)

        proj_ready = scaled_weights_lo(w_proj16[:, 1, :], w_proj32[:, :], w_proj16[:, 0, :], proj_hi)
        pool.wait(wo_in, gnorm_in)
        wo_ready = pool.mark(pool.engine.tensor_scalar(w_o_sb[:, :, :], w_o_sb[:, :, :], gnorm_sb[:, 0:1], None, ALU.mult))

        CHUNKS = VD // P
        rot_tmp = ring("rot_tmp", 2, [P, 2, 2 * T])
        rotated = ring("rotated", 2, [P, 2 * T])
        values = ring("values", 3, [P, TPS, VD])
        silu_gT = ring("silu_gT", 3, [P, CHUNKS, T])
        weights = ring("weights", 2, [P, HEADS, 3 * P])
        squaresT = sb("squaresT", [P, CHUNKS, T])
        gatedT = ring("gatedT", 2, [P, CHUNKS, T])
        norm_bias = sb("norm_bias", [P, 2 * TPS])
        BANK_OUT, BANK_ROWS, BANK_MIX = (0, 1), 2, 7
        BANK_QK, BANK_V, BANK_G = (3, 4), 5, 6
        BANK_SCORE = (3, 4, 5, 6)
        COL_X1, COL_X2, COL_HEAD = 0, TPS, 2 * TPS
        RS_N = COL_HEAD + TPS * HEADS
        (norm1, norm2, split1, split2, xT_ready, x2T_ready, qk_done, rot_ready, v_ready, g_ready, scored, masked, mixed,
         squared, heads_gated, projected_out, sums_done, sums_ready, attended) = ({} for _ in range(19))

        def add_first(b):
            tiles = [TPS * b + j for j in range(TPS)]
            added, stats = {}, {}

            def add(t):
                added[t] = add_back(0, t)

            def stat(t):
                dve.wait(added[t])
                stats[t] = dve.mark(dve.engine.bn_stats(row_stats[:, t, :], x_sb[:, t, :]))

            def aggregate(t):
                dve.wait(stats[t])
                stats[t] = dve.mark(dve.engine.bn_aggr(row_mean_var[:, t, :], row_stats[:, t, :]))

            return [lambda t=t, f=f: f(t) for f in (add, stat, aggregate) for t in tiles], lambda: stats[tiles[-1]]

        def normalise_on_act(b, buf, col, rs_ready, bias_read):
            bias = norm_bias[:, col:col + TPS]
            mean = row_mean_var[:, TPS * b:TPS * (b + 1), 0]
            dve.wait(rs_ready, bias_read)
            m = dve.mark(dve.engine.scalar_tensor_tensor(bias, mean, -1.0, rs_out[:, col:col + TPS], ALU.mult, ALU.mult))
            act.wait(m, xn32_read[buf])
            for j in range(TPS):
                m = act.mark(act.engine.activation(xn32[buf][:, j, :], x_sb[:, TPS * b + j, :], ACT.Identity,
                                                   bias=norm_bias[:, col + j:col + j + 1], scale=rs_out[:, col + j:col + j + 1]))
            return m

        def project_qk(b):
            span = slice(b * T, (b + 1) * T)
            hi, lo = xnT[:, 0, span], xnT[:, 1, span]
            pe.wait(xT_ready[b])
            for swapped in range(2):
                bank = banks[BANK_QK[swapped]]
                pe.wait(emptied[BANK_QK[swapped]])
                for j in range(2):
                    c = (2 * j + swapped) * P
                    w_hi, w_lo = w_proj16[:, 0, c:c + P], w_proj16[:, 1, c:c + P]
                    o = bank[:, j * T:(j + 1) * T]
                    pe.engine.matmul(o, w_hi, hi, start=True, stop=False)
                    pe.engine.matmul(o, w_hi, lo, start=False, stop=False)
                    m = pe.engine.matmul(o, w_lo, hi, start=False, stop=True)
                qk_done[b, swapped] = pe.mark(m)

        def rotate(b):
            tmp, r = rot_tmp[b % 2], rotated[b % 2]
            dve.wait(rot_ready.get(b - 2))
            for j in range(2):
                dve.wait(qk_done[b, j])
                m = dve.mark(dve.engine.tensor_tensor(tmp[:, j, :], banks[BANK_QK[j]][:, :], rope_sb[:, j * 2 * T:(j + 1) * 2 * T], ALU.mult))
                emptied[BANK_QK[j]] = m
            pool.wait(m, scored.get(b - 2))
            rot_ready[b] = pool.mark(pool.engine.tensor_tensor(r[:, :], tmp[:, 0, :], tmp[:, 1, :], ALU.add))

        def run_next(queue):
            if queue:
                queue.pop(0)()

        def project_vg(b, between):
            span = slice(b * T, (b + 1) * T)
            x_hi, x_lo = xnT[:, 0, span], xnT[:, 1, span]
            v_hi, v_lo = w_proj16[:, 0, 4 * P:4 * P + VD], w_proj16[:, 1, 4 * P:4 * P + VD]
            pe.wait(emptied[BANK_V])
            for j in range(TPS):
                hi, lo = x_hi[:, j * P:(j + 1) * P], x_lo[:, j * P:(j + 1) * P]
                o = banks[BANK_V][:, j * VD:(j + 1) * VD]
                pe.engine.matmul(o, hi, v_hi, start=True, stop=False)
                run_next(between)
                pe.engine.matmul(o, hi, v_lo, start=False, stop=False)
                run_next(between)
                m = pe.engine.matmul(o, lo, v_hi, start=False, stop=True)
            m = pe.mark(m)
            act.wait(m, mixed.get(b - 3))
            v_ready[b] = act.mark(act.engine.activation(values[b % 3][:, :, :].rearrange("p t c -> p (t c)"),
                                                        banks[BANK_V][:, :], ACT.Copy, scale=UNSCALE))
            emptied[BANK_V] = v_ready[b]
            pe.wait(emptied[BANK_G])
            for c in range(CHUNKS):
                cols = slice(4 * P + VD + c * P, 4 * P + VD + (c + 1) * P)
                w_hi, w_lo = w_proj16[:, 0, cols], w_proj16[:, 1, cols]
                o = banks[BANK_G][:, c * T:(c + 1) * T]
                pe.engine.matmul(o, w_hi, x_hi, start=True, stop=False)
                run_next(between)
                pe.engine.matmul(o, w_hi, x_lo, start=False, stop=False)
                m = pe.engine.matmul(o, w_lo, x_hi, start=False, stop=True)
            m = pe.mark(m)
            xnT_read[b] = m
            act.wait(m, heads_gated.get(b - 3))
            g_ready[b] = act.mark(act.engine.activation(silu_gT[b % 3][:, :, :].rearrange("p c t -> p (c t)"),
                                                        banks[BANK_G][:, :], ACT.Silu, scale=UNSCALE))
            emptied[BANK_G] = g_ready[b]

        def score(b, between):
            r = rotated[b % 2]
            pe.wait(rot_ready[b])
            for h in range(HEADS):
                hs = slice(h * DK, (h + 1) * DK)
                pe.wait(emptied[BANK_SCORE[h]])
                pe.engine.matmul(banks[BANK_SCORE[h]][:, 0:2 * P], r[hs, T:T + P], r[hs, 0:T], start=True, stop=True,
                                 tile_position=(h * DK, 0))
                if h == HEADS - 1:
                    run_next(between)
            for h in range(HEADS):
                hs = slice(h * DK, (h + 1) * DK)
                scored[b, h] = pe.mark(pe.engine.matmul(banks[BANK_SCORE[h]][:, 2 * P:3 * P], r[hs, T + P:2 * T], r[hs, P:T],
                                                        start=True, stop=True, tile_position=(h * DK, 0)))
                run_next(between)
            scored[b] = scored[b, HEADS - 1]

        def mask(b):

            def head(h):
                dve.wait(scored[b, h], mixed.get(b - 2) if h == 0 else None)
                m = dve.mark(dve.engine.tensor_tensor(weights[b % 2][:, h, :], banks[BANK_SCORE[h]][:, 0:3 * P], score_mask, ALU.mult))
                emptied[BANK_SCORE[h]] = masked[b, h] = m

            return [lambda h=h: head(h) for h in range(HEADS)]

        def mix(b):
            w, v, bank = weights[b % 2], values[b % 3], banks[BANK_MIX]
            pe.wait(v_ready[b], emptied[BANK_MIX])
            for h in range(HEADS):
                c, r = divmod(h, P // DV)
                rows, cols = slice(r * DV, (r + 1) * DV), slice(h * DV, (h + 1) * DV)
                at = (0, r * DV)
                q0, q1 = bank[rows, c * T:c * T + P], bank[rows, c * T + P:(c + 1) * T]
                pe.wait(masked[b, h])
                pe.engine.matmul(q0, v[:, 0, cols], w[:, h, 0:P], start=True, stop=True, tile_position=at)
                pe.engine.matmul(q1, v[:, 0, cols], w[:, h, P:2 * P], start=True, stop=False, tile_position=at)
                m = pe.engine.matmul(q1, v[:, 1, cols], w[:, h, 2 * P:3 * P], start=False, stop=True, tile_position=at)
            mixed[b] = pe.mark(m)

        def square_heads(b):
            bank = banks[BANK_MIX]
            act.wait(mixed[b], sums_done.get(b - 1))
            squared[b] = act.mark(act.engine.activation(squaresT[:, :, :].rearrange("p c t -> p (c t)"), bank[:, :], ACT.Square))

        def gate_heads(b):
            dve.wait(squared[b], g_ready[b], projected_out.get(b - 2))
            m = dve.mark(dve.engine.tensor_tensor(gatedT[b % 2][:, :, :].rearrange("p c t -> p (c t)"), banks[BANK_MIX][:, :],
                                                  silu_gT[b % 3][:, :, :].rearrange("p c t -> p (c t)"), ALU.mult))
            heads_gated[b] = emptied[BANK_MIX] = m

        def sum_matmuls(b):
            bank = banks[BANK_ROWS]
            width = P // DV * HEAD_COPIES

            def product(j, c):
                if j == 0 and c == 0:
                    pe.wait(squared[b], emptied[BANK_ROWS])
                m = pe.engine.matmul(bank[:, (j * CHUNKS + c) * width:(j * CHUNKS + c + 1) * width],
                                     squaresT[:, c, j * P:(j + 1) * P], head_rows, start=True, stop=True)
                if j == TPS - 1 and c == CHUNKS - 1:
                    sums_done[b] = pe.mark(m)

            return [lambda j=j, c=c: product(j, c) for j in range(TPS) for c in range(CHUNKS)]

        def sum_heads(b, val_read):
            act.wait(sums_done[b], val_read)
            sums = banks[BANK_ROWS][:, 0:TPS * HEADS * HEAD_COPIES].rearrange("p (g n) -> p g n", n=HEAD_COPIES)[:, :, 0]
            sums_ready[b] = act.mark(act.engine.activation(rs_val[:, COL_HEAD:RS_N], sums, ACT.Copy,
                                                           bias=EPS, scale=1.0 / DV))
            emptied[BANK_ROWS] = sums_ready[b]

        def project_out(b):
            gT = gatedT[b % 2]
            pe.wait(heads_gated[b], emptied[BANK_OUT[0]], emptied[BANK_OUT[1]])
            for c in range(CHUNKS):
                for j in range(TPS):
                    for r in range(P // DV):
                        rows = slice(r * DV, (r + 1) * DV)
                        col = (c * TPS + j) * D
                        m = pe.engine.matmul(banks[BANK_OUT[r]][:, col:col + D], gT[rows, c, j * P:(j + 1) * P],
                                             w_o_sb[rows, c, :], start=True, stop=True, tile_position=(r * DV, 0))
            projected_out[b] = pe.mark(m)

        def add_attention(b, rs_ready):
            dve.wait(rs_ready, projected_out[b])
            marks = [None] * TPS
            for h in range(HEADS):
                c, r = divmod(h, P // DV)
                for j in range(TPS):
                    t, col = TPS * b + j, (c * TPS + j) * D
                    dve.wait(marks[j])
                    marks[j] = dve.mark(dve.engine.scalar_tensor_tensor(
                        x_sb[:, t, :], banks[BANK_OUT[r]][:, col:col + D],
                        rs_out[:, COL_HEAD + j * HEADS + h:COL_HEAD + j * HEADS + h + 1], x_sb[:, t, :], ALU.mult, ALU.add))
            attended[b] = emptied[BANK_OUT[0]] = emptied[BANK_OUT[1]] = marks[-1]
            return layernorm_stats(range(TPS * b, TPS * (b + 1)), marks)

        ADD, NORM, PROJECT, SCORE, MIX, ATTEND, NORM2, GATES = range(8)

        def now(i, lag):
            return i - lag if 0 <= i - lag < SEQS else None

        out_tiles = out[NS * P:, :].rearrange("(t p) d -> p t d", p=P)

        def store_x(b):
            sp.wait_ge(*attended[b])
            return Counter(None, sem(f"x_stored{b}"), 16).mark(
                sp.dma_start(out_tiles[:, TPS * b:TPS * (b + 1), :], x_sb[:, TPS * b:TPS * (b + 1), :]))

        rows2_stored = []
        pool.wait(slots_ready, *results_stored)
        for j in range(TPS):
            fetch(0, j)
        pe.wait(proj_ready, wo_ready)
        dve.wait(rope_in, scores_ready)
        values_ready = []
        rs_free = [rs_free]
        act.engine.activation(table_out[:, :], b1_sb[:, 0:1], ACT.Silu)
        for i in range(SEQS + GATES):
            add, norm, proj, sc, mx, att, norm_2, gate = (now(i, lag) for lag in range(GATES + 1))
            if i + 1 < SEQS:
                for j in range(TPS):
                    fetch(0, TPS * (i + 1) + j)
            for m in values_ready:
                dve.wait(m)
            roots = rsqrt_steps(RS_N, None, rs_free) if values_ready else iter(())
            firsts, first_stats = add_first(add) if add is not None else ([], None)
            rs_ready, values_ready = None, []

            def norms():
                if norm is not None:
                    norm1[norm] = normalise_on_act(norm, norm % 2, COL_X1, rs_ready, norm1.get(norm - 1))
                if norm_2 is not None:
                    norm2[norm_2] = normalise_on_act(norm_2, 2 + norm_2 % 2, COL_X2, rs_ready, norm2.get(norm_2 - 1))
                if norm is not None:
                    split1[norm] = rows_lo(norm % 2, rows_hi(norm % 2, norm1[norm]), pool)
                if norm_2 is not None:
                    split2[norm_2] = rows_lo(2 + norm_2 % 2, rows_hi(2 + norm_2 % 2, norm2[norm_2]), pool)
                    rows2_stored.append(store_rows(1, norm_2, 2 + norm_2 % 2, split2[norm_2]))

            if mx is None:
                for m in roots:
                    rs_ready = m
                norms()
            for between in (mask(mx) if mx is not None else []) + firsts:
                rs_ready = next(roots, None) or rs_ready
                between()
            for m in roots:
                rs_ready = m
            if proj is not None:
                project_qk(proj)
            small = gate_matmuls(gate, x2T_ready[gate], gate_ready, BANK_ROWS) if gate is not None else []
            if proj is not None:
                project_vg(proj, small)
            for product in small:
                product()
            if gate is not None:
                logits_ready = gate_logits(gate, BANK_ROWS)
            if mx is not None:
                mix(mx)
                norms()
            if add is not None:
                values_ready.append(layernorm_value(COL_X1, TPS * add, TPS, first_stats(), rs_ready))
            attended_first = att is not None and proj is None
            if attended_first:
                m = add_attention(att, rs_ready)
                values_ready.append(layernorm_value(COL_X2, TPS * att, TPS, m, rs_ready))
                out_ready.append(store_x(att))
            if proj is not None:
                rotate(proj)
            if mx is not None:
                square_heads(mx)
                gate_heads(mx)
            small = sum_matmuls(mx) if mx is not None else []
            if sc is not None:
                score(sc, small)
            for product in small:
                product()
            if mx is not None:
                sum_heads(mx, rs_ready)
                values_ready.append(sums_ready[mx])
            if att is not None and not attended_first:
                m = add_attention(att, rs_ready)
                values_ready.append(layernorm_value(COL_X2, TPS * att, TPS, m, rs_ready))
                out_ready.append(store_x(att))
            if norm_2 is not None:
                x2T_ready[norm_2] = transpose_rows(norm_2, 2 + norm_2 % 2, split2[norm_2], BANK_MIX)
            if norm is not None:
                xT_ready[norm] = transpose_rows(norm, norm % 2, split1[norm], BANK_ROWS)
            if mx is not None:
                project_out(mx)
            if gate == SEQS - 2:
                choose(0, NT - TPS, logits_ready)
            rs_free = [m for m in (norm1.get(norm), norm2.get(norm_2), attended.get(att)) if m is not None] or [rs_ready]

        places_ready, scores_ready, tokens_ready, offsets_ready = route(1, *choose(NT - TPS, NT, logits_ready))
        results_stored = experts(1, rows2_stored, tokens_ready, offsets_ready, None, [], places_ready, out_ready,
                                 lambda: scores_of_slots(scores_ready))
        for m in results_stored:
            sp.wait_ge(*m)


def kernel(**inputs):
    import concourse.bacc as bacc
    from concourse.bass_utils import run_bass_kernel_spmd

    a = {k: np.asarray(v) for k, v in inputs.items()}
    swap = np.arange(P).reshape(HEADS, 2, DK // 2)[:, ::-1].reshape(-1)
    wq, wk = a["L0_attn_Wq"], a["L0_attn_Wk"]
    arrays = {
        "x": a["L0_attn_x"].reshape(TOKENS, D),
        "w_proj": np.concatenate([wq, wq[swap], wk, wk[swap], a["L0_attn_Wv"], a["L0_attn_Wg"]]).T,
        "w_o": a["L0_attn_Wo"].T,
        "gnorm": np.tile(a["L0_attn_gnorm_w"], 2).reshape(P, 1),
        "w_redT": a["L0_ffn_w_red"].T,
        "wg": a["L0_ffn_wg"],
        "w1": a["L0_ffn_w1"],
        "b1T": a["L0_ffn_b1"].reshape(E * NF, P).T,
        "w2": a["L0_ffn_w2"],
        "b2": a["L0_ffn_b2"],
        "rope": rope_tables(),
        "consts": small_constants(),
        "halves": half_constants(),
        "masks": causal_mask(),
    }
    arrays = {k: np.ascontiguousarray(v) for k, v in arrays.items()}
    nc = bacc.Bacc("TRN2", target_bir_lowering=False, num_devices=1)
    args = [nc.dram_tensor(f"in_{k}", v.shape, mybir.dt.from_np(v.dtype), kind="ExternalInput").ap()
            for k, v in arrays.items()]
    out = nc.dram_tensor("out_x", (NS * P + TOKENS, D), F32, kind="ExternalOutput").ap()
    macaron(nc, *args, out)
    r = run_bass_kernel_spmd(nc, [{f"in_{k}": v for k, v in arrays.items()}], core_ids=[0])
    return r.results[0]["out_x"][NS * P:].reshape(SEQS, T, D)
```
